# Optimizing a Trainium2 kernel written in Bass

```python
import numpy as np
import jax
import jax.numpy as jnp

def _softmax(x, axis=-1):
    return jax.nn.softmax(x, axis=axis)

def _gelu(x):
    return jax.nn.gelu(x, approximate=True)

def _silu(x):
    return jax.nn.silu(x)

def _sigmoid(x):
    return jax.nn.sigmoid(x)

def _layernorm(x, axis=-1, eps=1e-05):
    m = jnp.mean(x, axis=axis, keepdims=True)
    v = jnp.var(x, axis=axis, keepdims=True)
    return (x - m) / jnp.sqrt(v + eps)

def _scatter_add(tgt, idx, src, axis=0):
    return tgt.at[idx].add(src)

def _segment_sum(src, seg, n):
    return jax.ops.segment_sum(src, seg, n)
kernel_name = 'mk_dlrm_tower_d1_rec_r8_5bc315'

def setup_inputs(seed: int=0):
    np.random.seed(seed)
    _w = jnp.asarray

    def _rec_inputs():
        import jax
        import jax.numpy as jnp
        _tk = jax.random.key(seed)
        ids = jnp.stack([jax.random.randint(jax.random.fold_in(_tk, 200 + f), (512,), 0, v, jnp.int32) for f, v in enumerate([12500, 1000, 1250, 12500, 125000, 1250, 12500, 12500, 1250, 1000, 1000, 1000, 1250, 1250, 1250, 1000, 1250, 12500, 1250, 1250, 1250, 1000, 1000, 1250, 1250, 1000])], axis=1)
        tbl_0 = 0.05 * jax.random.normal(jax.random.fold_in(_tk, 500 + 0), (12500, 128), jnp.float32)
        tbl_1 = 0.05 * jax.random.normal(jax.random.fold_in(_tk, 500 + 1), (1000, 128), jnp.float32)
        tbl_2 = 0.05 * jax.random.normal(jax.random.fold_in(_tk, 500 + 2), (1250, 128), jnp.float32)
        tbl_3 = 0.05 * jax.random.normal(jax.random.fold_in(_tk, 500 + 3), (12500, 128), jnp.float32)
        tbl_4 = 0.05 * jax.random.normal(jax.random.fold_in(_tk, 500 + 4), (125000, 128), jnp.float32)
        tbl_5 = 0.05 * jax.random.normal(jax.random.fold_in(_tk, 500 + 5), (1250, 128), jnp.float32)
        tbl_6 = 0.05 * jax.random.normal(jax.random.fold_in(_tk, 500 + 6), (12500, 128), jnp.float32)
        tbl_7 = 0.05 * jax.random.normal(jax.random.fold_in(_tk, 500 + 7), (12500, 128), jnp.float32)
        tbl_8 = 0.05 * jax.random.normal(jax.random.fold_in(_tk, 500 + 8), (1250, 128), jnp.float32)
        tbl_9 = 0.05 * jax.random.normal(jax.random.fold_in(_tk, 500 + 9), (1000, 128), jnp.float32)
        tbl_10 = 0.05 * jax.random.normal(jax.random.fold_in(_tk, 500 + 10), (1000, 128), jnp.float32)
        tbl_11 = 0.05 * jax.random.normal(jax.random.fold_in(_tk, 500 + 11), (1000, 128), jnp.float32)
        tbl_12 = 0.05 * jax.random.normal(jax.random.fold_in(_tk, 500 + 12), (1250, 128), jnp.float32)
        tbl_13 = 0.05 * jax.random.normal(jax.random.fold_in(_tk, 500 + 13), (1250, 128), jnp.float32)
        tbl_14 = 0.05 * jax.random.normal(jax.random.fold_in(_tk, 500 + 14), (1250, 128), jnp.float32)
        tbl_15 = 0.05 * jax.random.normal(jax.random.fold_in(_tk, 500 + 15), (1000, 128), jnp.float32)
        tbl_16 = 0.05 * jax.random.normal(jax.random.fold_in(_tk, 500 + 16), (1250, 128), jnp.float32)
        tbl_17 = 0.05 * jax.random.normal(jax.random.fold_in(_tk, 500 + 17), (12500, 128), jnp.float32)
        tbl_18 = 0.05 * jax.random.normal(jax.random.fold_in(_tk, 500 + 18), (1250, 128), jnp.float32)
        tbl_19 = 0.05 * jax.random.normal(jax.random.fold_in(_tk, 500 + 19), (1250, 128), jnp.float32)
        tbl_20 = 0.05 * jax.random.normal(jax.random.fold_in(_tk, 500 + 20), (1250, 128), jnp.float32)
        tbl_21 = 0.05 * jax.random.normal(jax.random.fold_in(_tk, 500 + 21), (1000, 128), jnp.float32)
        tbl_22 = 0.05 * jax.random.normal(jax.random.fold_in(_tk, 500 + 22), (1000, 128), jnp.float32)
        tbl_23 = 0.05 * jax.random.normal(jax.random.fold_in(_tk, 500 + 23), (1250, 128), jnp.float32)
        tbl_24 = 0.05 * jax.random.normal(jax.random.fold_in(_tk, 500 + 24), (1250, 128), jnp.float32)
        tbl_25 = 0.05 * jax.random.normal(jax.random.fold_in(_tk, 500 + 25), (1000, 128), jnp.float32)
        _rk = jax.random.fold_in(_tk, 7)
        r_dense_features = -0.000520686 + 1.00062 * jax.random.normal(jax.random.fold_in(_rk, 101), (512, 128), jnp.float32)
        W_top1 = 0.0405887 * jax.random.normal(jax.random.fold_in(_tk, 801), (607, 512), jnp.float32)
        W_top2 = 0.0441942 * jax.random.normal(jax.random.fold_in(_tk, 802), (512, 256), jnp.float32)
        W_top3 = 0.0625 * jax.random.normal(jax.random.fold_in(_tk, 803), (256, 1), jnp.float32)
        b_top1 = jnp.zeros((512,), jnp.float32)
        b_top2 = jnp.zeros((256,), jnp.float32)
        return (r_dense_features, ids, tbl_0, tbl_1, tbl_2, tbl_3, tbl_4, tbl_5, tbl_6, tbl_7, tbl_8, tbl_9, tbl_10, tbl_11, tbl_12, tbl_13, tbl_14, tbl_15, tbl_16, tbl_17, tbl_18, tbl_19, tbl_20, tbl_21, tbl_22, tbl_23, tbl_24, tbl_25, W_top1, b_top1, W_top2, b_top2, W_top3)
    r_dense_features, ids, tbl_0, tbl_1, tbl_2, tbl_3, tbl_4, tbl_5, tbl_6, tbl_7, tbl_8, tbl_9, tbl_10, tbl_11, tbl_12, tbl_13, tbl_14, tbl_15, tbl_16, tbl_17, tbl_18, tbl_19, tbl_20, tbl_21, tbl_22, tbl_23, tbl_24, tbl_25, W_top1, b_top1, W_top2, b_top2, W_top3 = _rec_inputs()

    def _L0_rec_setup():
        import jax, jax.numpy as jnp
        import numpy as np
        NUM_SPARSE = 26
        EMBED_DIM = 128
        BATCH = 2048
        key = jax.random.key(seed)
        k1, k2 = jax.random.split(key)
        dense_features = jax.random.normal(k1, (BATCH, EMBED_DIM), dtype=jnp.float32)
        sparse_features = jax.random.normal(k2, (BATCH, NUM_SPARSE, EMBED_DIM), dtype=jnp.float32)
        return {'dense_features': dense_features, 'sparse_features': sparse_features}
    _L0_rec_all = _L0_rec_setup()
    _L0_rec_in = {k: v for k, v in _L0_rec_all.items() if k in ()}
    del _L0_rec_all
    return {'r_dense_features': r_dense_features, 'ids': ids, 'tbl_0': tbl_0, 'tbl_1': tbl_1, 'tbl_2': tbl_2, 'tbl_3': tbl_3, 'tbl_4': tbl_4, 'tbl_5': tbl_5, 'tbl_6': tbl_6, 'tbl_7': tbl_7, 'tbl_8': tbl_8, 'tbl_9': tbl_9, 'tbl_10': tbl_10, 'tbl_11': tbl_11, 'tbl_12': tbl_12, 'tbl_13': tbl_13, 'tbl_14': tbl_14, 'tbl_15': tbl_15, 'tbl_16': tbl_16, 'tbl_17': tbl_17, 'tbl_18': tbl_18, 'tbl_19': tbl_19, 'tbl_20': tbl_20, 'tbl_21': tbl_21, 'tbl_22': tbl_22, 'tbl_23': tbl_23, 'tbl_24': tbl_24, 'tbl_25': tbl_25, 'W_top1': W_top1, 'b_top1': b_top1, 'W_top2': W_top2, 'b_top2': b_top2, 'W_top3': W_top3}

def reference(r_dense_features, ids, tbl_0, tbl_1, tbl_2, tbl_3, tbl_4, tbl_5, tbl_6, tbl_7, tbl_8, tbl_9, tbl_10, tbl_11, tbl_12, tbl_13, tbl_14, tbl_15, tbl_16, tbl_17, tbl_18, tbl_19, tbl_20, tbl_21, tbl_22, tbl_23, tbl_24, tbl_25, W_top1, b_top1, W_top2, b_top2, W_top3):
    import jax
    import jax.numpy as jnp

    def _L0_rec_ref(dense_features, sparse_features):
        import jax, jax.numpy as jnp
        import numpy as np
        NUM_SPARSE = 26
        EMBED_DIM = 128
        BATCH = 2048
        F = NUM_SPARSE + 1
        combined = jnp.concatenate([dense_features[:, None, :], sparse_features], axis=1)
        interactions = jnp.einsum('bfd,bgd->bfg', combined, combined)
        iu, ju = jnp.triu_indices(F, k=1)
        interactions_flat = interactions[:, iu, ju]
        return jnp.concatenate([dense_features, interactions_flat], axis=1)
    e = jnp.stack([tbl_0[ids[:, 0]], tbl_1[ids[:, 1]], tbl_2[ids[:, 2]], tbl_3[ids[:, 3]], tbl_4[ids[:, 4]], tbl_5[ids[:, 5]], tbl_6[ids[:, 6]], tbl_7[ids[:, 7]], tbl_8[ids[:, 8]], tbl_9[ids[:, 9]], tbl_10[ids[:, 10]], tbl_11[ids[:, 11]], tbl_12[ids[:, 12]], tbl_13[ids[:, 13]], tbl_14[ids[:, 14]], tbl_15[ids[:, 15]], tbl_16[ids[:, 16]], tbl_17[ids[:, 17]], tbl_18[ids[:, 18]], tbl_19[ids[:, 19]], tbl_20[ids[:, 20]], tbl_21[ids[:, 21]], tbl_22[ids[:, 22]], tbl_23[ids[:, 23]], tbl_24[ids[:, 24]], tbl_25[ids[:, 25]]], axis=1)
    z = _L0_rec_ref(r_dense_features, e)
    z = z.reshape(z.shape[0], -1)
    h = jnp.concatenate([z, r_dense_features], axis=1)
    h = jnp.maximum(h @ W_top1 + b_top1, 0.0)
    h = jnp.maximum(h @ W_top2 + b_top2, 0.0)
    y = h @ W_top3
    return y

_drawn_inputs = setup_inputs


def setup_inputs(seed=0):
    import zlib

    import numpy as np

    out = dict(_drawn_inputs(seed))
    spreads = {'b_top1': (0.0, 0.1), 'b_top2': (0.0, 0.1)}
    factors = {}
    for name, (base, spread) in spreads.items():
        noise = np.random.default_rng([zlib.crc32(name.encode()), seed]).standard_normal(out[name].shape)
        drawn = base * np.exp(spread * noise) if base else spread * noise
        out[name] = jnp.asarray(drawn.astype(out[name].dtype))
    for name, factor in factors.items():
        out[name] = (out[name] * factor).astype(out[name].dtype)
    return out
```

```python
import concourse.bass as bass
from concourse import mybir
from contextlib import ExitStack

F32 = mybir.dt.float32
F32R = mybir.dt.float32r
I32 = mybir.dt.int32
ACT = mybir.ActivationFunctionType
ALU = mybir.AluOpType

P = 128
B = 512
TILES = B // P
ROWS = [12500, 1000, 1250, 12500, 125000, 1250, 12500, 12500, 1250, 1000, 1000, 1000, 1250,
        1250, 1250, 1000, 1250, 12500, 1250, 1250, 1250, 1000, 1000, 1250, 1250, 1000]
NTAB = len(ROWS)
NF = NTAB + 1
SLOTS = 32

ONE_HOT = [1, 9, 10, 11, 15, 21, 22, 25, 2]
GATHERED = [f for f in range(NTAB) if f not in ONE_HOT]
KP = 125
CHUNKS = [ROWS[f] // KP for f in ONE_HOT]
MAXC = max(CHUNKS)
CHUNK0 = [sum(CHUNKS[:i]) for i in range(len(ONE_HOT) + 1)]
NOH, NG = len(ONE_HOT), len(GATHERED)
SLOT_FEATURE = [0] + [f + 1 for f in GATHERED] + [f + 1 for f in ONE_HOT]

GROUP = 4
GROUPS = [list(range(a, min(a + GROUP, NG))) for a in range(0, NG, GROUP)]
NGR = len(GROUPS)

NG_COL = NF - 1
QUADS = P // 32
Q = P // QUADS
CHUNK_Q = 8
NCH = Q // CHUNK_Q
BLOCKS = [(0, 4), (4, 4), (8, 4), (12, 4), (16, 4), (20, 2), (22, 2), (24, 2)]
BLOCK_OFF = [sum(n * (NF - 1 - g) for g, n in BLOCKS[:i]) for i in range(len(BLOCKS) + 1)]
NPAIR = BLOCK_OFF[-1]
KT = NPAIR // P
assert KT * P == NPAIR
BANKS2 = [[0], [1], [2], [3], [4], [5, 6], [7]]
NB2 = len(BANKS2)
H1, H2 = 512, 256
N1, N2 = H1 // P, H2 // P
K1 = KT + 1

OH_RING, IDS_RING = 8, 4


def pair_rows_of_w1():
    rows = []
    for g0, n in BLOCKS:
        for g in range(g0, g0 + n):
            for f in range(g0 + 1, NF):
                if f <= g:
                    rows.append(None)
                    continue
                i, j = sorted((SLOT_FEATURE[g], SLOT_FEATURE[f]))
                rows.append(P + i * NF - i * (i + 1) // 2 + (j - i - 1))
    return rows


LATE = NOH - (NGR - 1)


def table_fill(i):
    return 1 + i + max(0, i - LATE)


def group_fill(t, g):
    if t == 0:
        return table_fill(LATE + g) + 1 if g < NGR - 1 else NOH + NGR
    return 1 + NOH + t * NGR + g


def group_on_act(t, g):
    return g % 2 == 1


def fills_by(act):
    order = {0: True}
    order |= {table_fill(i): True for i in range(NOH)}
    order |= {group_fill(t, g): group_on_act(t, g) for t in range(TILES) for g in range(NGR)}
    assert sorted(order) == list(range(len(order)))
    return [u for u in sorted(order) if order[u] == act]


ACT_FILLS, DVE_FILLS = fills_by(True), fills_by(False)



def late_fills():
    order = []
    for t in range(TILES):
        if t:
            order.append(("l1", t - 1))
        order += [("pair", t, k) for k in range(NB2)]
        if t:
            order += [("l2", t - 1), ("l3", t - 1)]
        order.append(("turn", t))
    t = TILES - 1
    order += [("l1", t), ("l2", t), ("l3", t)]
    return {what: n for n, what in enumerate(order)}


LATE_FILL = late_fills()


def late_on_act(what):
    return what[0] == "l2" or (what[0] == "pair" and what[2] % 2 == 0)


LATE_ACT = [n for w, n in LATE_FILL.items() if late_on_act(w)]
LATE_DVE = [n for w, n in LATE_FILL.items() if not late_on_act(w)]


def build(nc, dense, ids_rows, ids_bcast, tables, w1, b1, w2, b2, w3, out):
    with ExitStack() as ctx:
        def sb(name, shape, dt=F32):
            return ctx.enter_context(nc.sbuf_tensor(name, shape, dt))

        def sem(name):
            return ctx.enter_context(nc.semaphore(name))

        idx = sb("idx", [P, TILES, NTAB], I32)
        ids = sb("ids", [P, IDS_RING, B], I32)
        row0 = {c: sb(f"row_of_partition_{c}", [P, c]) for c in sorted(set(CHUNKS))}
        x_rows = sb("x_rows", [P, TILES, P])
        e_rows = sb("e_rows", [P, 2, NG, P])
        table = sb("table", [P, 2, MAXC, P])
        table_hi = sb("table_hi", [P, 2, MAXC, P], F32R)
        table_lo = sb("table_lo", [P, 2, MAXC, P], F32R)
        onehot = sb("onehot", [P, OH_RING, B], F32R)
        eT = sb("eT", [P, B, SLOTS])
        x_hi = sb("x_hi", [P, B], F32R)
        x_lo = sb("x_lo", [P, B], F32R)
        dots = sb("dots", [P, NG_COL, Q])
        pair_rows = sb("pair_rows", [Q, QUADS, NPAIR])
        pT_hi = sb("pT_hi", [P, KT, P], F32R)
        pT_lo = sb("pT_lo", [P, KT, P], F32R)
        w1_raw = sb("w1_raw", [P, K1 + 1, H1])
        w1_hi = sb("w1_hi", [P, K1, H1], F32R)
        w1_lo = sb("w1_lo", [P, K1, H1], F32R)
        w2_raw = sb("w2_raw", [P, N1, H2])
        w2_hi = sb("w2_hi", [P, N1, H2], F32R)
        w2_lo = sb("w2_lo", [P, N1, H2], F32R)
        w3_sb = sb("w3_sb", [P, N2])
        bias_raw = sb("bias_raw", [1, H1 + H2])
        bias = sb("bias", [P, H1 + H2], F32R)
        ones = sb("ones", [P, P], F32R)
        h1_hi = sb("h1_hi", [P, N1, P], F32R)
        h1_lo = sb("h1_lo", [P, N1, P], F32R)
        h2 = sb("h2", [P, N2, P])
        y = sb("y", [1, B])
        ident = sb("ident", [P, P])
        one_col = sb("one_col", [P, P])

        look = ctx.enter_context(nc.psum_tensor("look", [P, 2, B], F32))
        gram = ctx.enter_context(nc.psum_tensor("gram", [P, 2, CHUNK_Q, P], F32))
        late = ctx.enter_context(nc.psum_tensor("late", [P, 2, B], F32))

        idx_in = sem("idx_in")
        ids_in = [sem(f"ids_in{k}") for k in range(IDS_RING)]
        table_in = [sem(f"table_in{k}") for k in range(2)]
        x_in = sem("x_in")
        w_in = sem("w_in")
        rows_in = [[sem(f"rows_in{t}_{g}") for g in range(NGR)] for t in range(TILES)]
        y_out = sem("y_out")
        ident_ready = sem("ident_ready")
        row0_ready = sem("row0_ready")
        pads_ready = sem("pads_ready")
        hi_ready = sem("hi_ready")
        lo_ready = sem("lo_ready")
        onehot_ready = sem("onehot_ready")
        onehot_used = sem("onehot_used")
        look_full = sem("look_full")
        eT_act = sem("eT_act")
        eT_dve = sem("eT_dve")
        x_hi_ready = sem("x_hi_ready")
        x_lo_ready = sem("x_lo_ready")
        w_sum = sem("w_sum")
        w_hi = sem("w_hi")
        w_lo = sem("w_lo")
        gram_full = sem("gram_full")
        dots_act = sem("dots_act")
        dots_dve = sem("dots_dve")
        late_full = sem("late_full")
        late_act = sem("late_act")
        late_dve = sem("late_dve")
        pT_hi_ready = sem("pT_hi_ready")
        h1_hi_ready = sem("h1_hi_ready")

        block = ctx.enter_context(nc.Block())

        def wait_looked_up(eng, u):
            if u in ACT_FILLS:
                eng.wait_ge(eT_act, ACT_FILLS.index(u) + 1)
            else:
                eng.wait_ge(eT_dve, DVE_FILLS.index(u) + 1)
            if u == 0:
                eng.wait_ge(x_lo_ready, 1)

        def wait_late(eng, n):
            if n in LATE_ACT:
                eng.wait_ge(late_act, LATE_ACT.index(n) + 1)
            else:
                eng.wait_ge(late_dve, LATE_DVE.index(n) + 1)

        @block.sync
        def _(sp):
            def load_table(i):
                c = CHUNKS[i]
                if i >= 2:
                    sp.wait_ge(lo_ready, i - 1)
                sp.dma_start(table[0:KP, i % 2, 0:c, :],
                             tables[ONE_HOT[i]].rearrange("(p c) d -> p c d", c=c)).then_inc(table_in[i % 2], 16)

            def load_ids(i):
                if i >= IDS_RING:
                    sp.wait_ge(onehot_ready, CHUNK0[i - IDS_RING + 1])
                sp.dma_start(ids[:, i % IDS_RING, :],
                             ids_bcast[ONE_HOT[i]:ONE_HOT[i] + 1, :].to_broadcast([P, B])
                             ).then_inc(ids_in[i % IDS_RING], 16)

            sp.dma_start(idx[:, :, :], ids_rows).then_inc(idx_in, 16)
            load_ids(0)
            load_table(0)
            load_ids(1)
            load_table(1)
            sp.dma_start(x_rows[:, :, :], dense.rearrange("(t p) d -> p t d", p=P)).then_inc(x_in, 16)
            load_ids(2)
            load_ids(3)
            for i in range(2, NOH):
                load_table(i)
                if i + 2 < NOH:
                    load_ids(i + 2)
                if i == 3:
                    sp.dma_start(w1_raw[:, :, :], w1).then_inc(w_in, 16)
                    sp.dma_start(w2_raw[:, :, :], w2).then_inc(w_in, 16)
                    sp.dma_start(bias_raw[:, 0:H1], b1).then_inc(w_in, 16)
                    sp.dma_start(bias_raw[:, H1:H1 + H2], b2).then_inc(w_in, 16)
                    sp.dma_start(w3_sb[:, :], w3).then_inc(w_in, 16)
            wait_late(sp, LATE_FILL["l3", TILES - 1])
            sp.dma_start(out, y[:, :]).then_inc(y_out, 16)
            sp.wait_ge(y_out, 16)

        @block.gpsimd
        def _(pool):
            for c in sorted(row0):
                pool.iota(row0[c][:, :], pattern=[[1, c]], base=0, channel_multiplier=c,
                          allow_small_or_imprecise_dtypes=True).then_inc(row0_ready, 1)
            pool.memset(one_col[:, :], 1.0).then_inc(ident_ready, 1)
            pool.wait_ge(ident_ready, 1)
            pool.affine_select(out=ident[:, :], in_=one_col[:, :], compare_op=ALU.is_equal, fill=0.0,
                               base=0, pattern=[[-1, P]], channel_multiplier=1).then_inc(ident_ready, 1)
            pool.wait_ge(idx_in, 16)
            for t in range(TILES):
                for g in range(NGR):
                    if t >= 2:
                        pool.wait_ge(look_full, group_fill(t - 2, g) + 1)
                    for s in GROUPS[g]:
                        f = GATHERED[s]
                        pool.indirect_dma_start(
                            out=e_rows[:, t % 2, s, :], out_offset=None, in_=tables[f][:, :],
                            in_offset=bass.IndirectOffsetOnAxis(ap=idx[:, t, f:f + 1], axis=0)
                        ).then_inc(rows_in[t][g], 16)

        @block.tensor
        def _(pe):
            def turn_dense():
                pe.wait_ge(ident_ready, 2)
                pe.wait_ge(x_in, 16)
                for t in range(TILES):
                    last = pe.transpose(look[:, 0, t * P:(t + 1) * P], x_rows[:, t, :], ident[:, :])
                last.then_inc(look_full, 1)

            def one_hot_product(i):
                u = table_fill(i)
                if u >= 2:
                    wait_looked_up(pe, u - 2)
                pe.wait_ge(hi_ready, i + 1)
                pe.wait_ge(lo_ready, i + 1)
                for c in range(CHUNKS[i]):
                    n = CHUNK0[i] + c
                    pe.wait_ge(onehot_ready, n + 1)
                    pe.matmul(look[:, u % 2, :], table_hi[0:KP, i % 2, c, :], onehot[0:KP, n % OH_RING, :],
                              start=c == 0, stop=False)
                    last = pe.matmul(look[:, u % 2, :], table_lo[0:KP, i % 2, c, :],
                                     onehot[0:KP, n % OH_RING, :], start=False, stop=c == CHUNKS[i] - 1)
                    if c < CHUNKS[i] - 1:
                        last.then_inc(onehot_used, 1)
                last.then_inc(look_full, 1)

            def turn_group(t, g):
                u = group_fill(t, g)
                wait_looked_up(pe, u - 2)
                pe.wait_ge(rows_in[t][g], 16 * len(GROUPS[g]))
                for k, s in enumerate(GROUPS[g]):
                    last = pe.transpose(look[:, u % 2, k * P:(k + 1) * P], e_rows[:, t % 2, s, :], ident[:, :])
                last.then_inc(look_full, 1)

            def gram_tile(t):
                pe.wait_ge(eT_act, len([u for u in ACT_FILLS if u <= group_fill(t, NGR - 1)]))
                pe.wait_ge(eT_dve, len([u for u in DVE_FILLS if u <= group_fill(t, NGR - 1)]))
                if t == 0:
                    pe.wait_ge(pads_ready, 1)
                for c in range(NCH):
                    n = t * NCH + c
                    if n >= 2:
                        pe.wait_ge(dots_act, n - 1)
                        pe.wait_ge(dots_dve, n - 1)
                    for q in range(CHUNK_Q):
                        b = t * P + (c * CHUNK_Q + q) * QUADS
                        last = pe.matmul(gram[:, n % 2, q, 0:QUADS * NG_COL], eT[:, b:b + QUADS, :],
                                         eT[:, b:b + QUADS, 0:NG_COL], start=True, stop=True)
                    last.then_inc(gram_full, 1)

            def late_bank(what):
                n = LATE_FILL[what]
                if n >= 2:
                    wait_late(pe, n - 2)
                return late[:, n % 2, :]

            def pairs_tile(t):
                pe.wait_ge(dots_act, (t + 1) * NCH)
                pe.wait_ge(dots_dve, (t + 1) * NCH)
                for k, blocks in enumerate(BANKS2):
                    bank = late_bank(("pair", t, k))
                    g0, g1 = BLOCKS[blocks[0]][0], sum(BLOCKS[blocks[-1]])
                    for g in range(g0, g1):
                        last = pe.transpose(bank[0:Q, (g - g0) * P:(g - g0 + 1) * P], dots[:, g, :], ident[:, :])
                    last.then_inc(late_full, 1)

            def turn_pairs(t):
                bank = late_bank(("turn", t))
                for k in range(NB2):
                    wait_late(pe, LATE_FILL["pair", t, k])
                for k in range(KT):
                    for j in range(QUADS):
                        at = k * P + j * Q
                        last = pe.transpose(bank[:, at:at + Q], pair_rows[:, j, k * P:(k + 1) * P],
                                            ident[0:Q, 0:Q])
                last.then_inc(late_full, 1)

            def layer1(t):
                bank = late_bank(("l1", t))
                if t == 0:
                    pe.wait_ge(w_hi, 3)
                    pe.wait_ge(w_lo, 3)
                wait_late(pe, LATE_FILL["turn", t])
                cols = slice(t * P, (t + 1) * P)
                for n in range(N1):
                    o = bank[:, n * P:(n + 1) * P]
                    rows = slice(n * P, (n + 1) * P)
                    pe.matmul(o, bias[:, rows], ones[:, :], start=True, stop=False)
                    for k in range(K1):
                        hi = pT_hi[:, k, :] if k < KT else x_hi[:, cols]
                        lo = pT_lo[:, k, :] if k < KT else x_lo[:, cols]
                        pe.matmul(o, w1_hi[:, k, rows], hi, start=False, stop=False)
                        pe.matmul(o, w1_hi[:, k, rows], lo, start=False, stop=False)
                        last = pe.matmul(o, w1_lo[:, k, rows], hi, start=False, stop=k == K1 - 1)
                last.then_inc(late_full, 1)

            def layer2(t):
                bank = late_bank(("l2", t))
                wait_late(pe, LATE_FILL["l1", t])
                for n in range(N2):
                    o = bank[:, n * P:(n + 1) * P]
                    rows = slice(n * P, (n + 1) * P)
                    pe.matmul(o, bias[:, H1 + n * P:H1 + (n + 1) * P], ones[:, :], start=True, stop=False)
                    for k in range(N1):
                        pe.matmul(o, w2_hi[:, k, rows], h1_hi[:, k, :], start=False, stop=False)
                        pe.matmul(o, w2_hi[:, k, rows], h1_lo[:, k, :], start=False, stop=False)
                        last = pe.matmul(o, w2_lo[:, k, rows], h1_hi[:, k, :], start=False, stop=k == N1 - 1)
                last.then_inc(late_full, 1)

            def layer3(t):
                bank = late_bank(("l3", t))
                wait_late(pe, LATE_FILL["l2", t])
                for k in range(N2):
                    last = pe.matmul(bank[0:1, 0:P], w3_sb[:, k:k + 1], h2[:, k, :], start=k == 0, stop=k == N2 - 1)
                last.then_inc(late_full, 1)

            turn_dense()
            for i in range(NOH):
                one_hot_product(i)
                if i >= LATE:
                    turn_group(0, i - LATE)
            turn_group(0, NGR - 1)
            for t in range(TILES):
                if t:
                    for g in range(NGR):
                        turn_group(t, g)
                gram_tile(t)
                if t:
                    layer1(t - 1)
                pairs_tile(t)
                if t:
                    layer2(t - 1)
                    layer3(t - 1)
                turn_pairs(t)
            layer1(TILES - 1)
            layer2(TILES - 1)
            layer3(TILES - 1)

        def group_copy(eng, copy, t, g, done):
            u = group_fill(t, g)
            n = len(GROUPS[g])
            eng.wait_ge(look_full, u + 1)
            s = 1 + GROUPS[g][0]
            copy(eT[:, t * P:(t + 1) * P, s:s + n].rearrange("d b f -> d f b"),
                 look[:, u % 2, 0:n * P].rearrange("d (f b) -> d f b", f=n)).then_inc(done, 1)

        def dots_copy(copy, t, c, j):
            n = t * NCH + c
            rows = slice(32 * j, 32 * j + 32)
            return copy(dots[rows, :, c * CHUNK_Q:(c + 1) * CHUNK_Q].rearrange("f g q -> f q g"),
                        gram[rows, n % 2, :, j * NG_COL:(j + 1) * NG_COL])

        def pair_copy(copy, t, k):
            n = LATE_FILL["pair", t, k]
            first = BLOCKS[BANKS2[k][0]][0]
            for blk in BANKS2[k]:
                g0, ng = BLOCKS[blk]
                w = NF - 1 - g0
                src = late[0:Q, n % 2, (g0 - first) * P:(g0 - first + ng) * P].rearrange(
                    "q (g j f) -> q g j f", g=ng, j=QUADS)[:, :, :, g0 + 1:NF]
                dst = pair_rows[:, :, BLOCK_OFF[blk]:BLOCK_OFF[blk + 1]].rearrange(
                    "q j (g w) -> q g j w", g=ng)
                last = copy(dst, src)
            return last

        @block.scalar
        def _(act):
            def copy(dst, src):
                return act.activation(dst, src, ACT.Copy)

            def split_hi(i):
                act.wait_ge(table_in[i % 2], 16 * (i // 2 + 1))
                if i >= 2:
                    act.wait_ge(look_full, table_fill(i - 2) + 1)
                c = CHUNKS[i]
                copy(table_hi[0:KP, i % 2, 0:c, :], table[0:KP, i % 2, 0:c, :]).then_inc(hi_ready, 1)

            def table_copy(i):
                u = table_fill(i)
                act.wait_ge(look_full, u + 1)
                copy(eT[:, :, 1 + NG + i], look[:, u % 2, :]).then_inc(eT_act, 1)

            split_hi(0)
            split_hi(1)
            act.wait_ge(look_full, 1)
            copy(eT[:, :, 0], look[:, 0, :]).then_inc(eT_act, 1)
            copy(x_hi[:, :], look[:, 0, :]).then_inc(x_hi_ready, 1)
            for i in range(NOH):
                table_copy(i)
                if i + 2 < NOH:
                    split_hi(i + 2)
                if i >= LATE and group_on_act(0, i - LATE):
                    group_copy(act, copy, 0, i - LATE, eT_act)
                if i == NOH - 2:
                    act.wait_ge(w_in, 16 * 5)
                    act.wait_ge(pads_ready, 1)
                    copy(bias[0:1, :], bias_raw[:, :]).then_inc(w_hi, 1)
                    act.wait_ge(w_sum, 1)
                    copy(w1_hi[:, :, :], w1_raw[:, 0:K1, :]).then_inc(w_hi, 1)
                    copy(w2_hi[:, :, :], w2_raw[:, :, :]).then_inc(w_hi, 1)
            if group_on_act(0, NGR - 1):
                group_copy(act, copy, 0, NGR - 1, eT_act)

            def h1_split(t):
                n = LATE_FILL["l1", t]
                act.wait_ge(late_full, n + 1)
                if t:
                    act.wait_ge(late_full, LATE_FILL["l2", t - 1] + 1)
                act.activation(h1_hi[:, :, :], late[:, n % 2, :].rearrange("n (k b) -> n k b", k=N1),
                               ACT.Relu).then_inc(h1_hi_ready, 1)

            def h2_relu(t):
                n = LATE_FILL["l2", t]
                act.wait_ge(late_full, n + 1)
                if t:
                    act.wait_ge(late_full, LATE_FILL["l3", t - 1] + 1)
                act.activation(h2[:, :, :], late[:, n % 2, 0:N2 * P].rearrange("n (k b) -> n k b", k=N2),
                               ACT.Relu).then_inc(late_act, 1)

            for t in range(TILES):
                if t:
                    for g in range(NGR):
                        if group_on_act(t, g):
                            group_copy(act, copy, t, g, eT_act)
                    act.wait_ge(late_full, LATE_FILL["pair", t - 1, NB2 - 1] + 1)
                for c in range(NCH):
                    act.wait_ge(gram_full, t * NCH + c + 1)
                    dots_copy(copy, t, c, 0)
                    dots_copy(copy, t, c, 1).then_inc(dots_act, 1)
                if t:
                    h1_split(t - 1)
                    act.wait_ge(late_full, LATE_FILL["turn", t - 1] + 1)
                for k in range(NB2):
                    if late_on_act(("pair", t, k)):
                        act.wait_ge(late_full, LATE_FILL["pair", t, k] + 1)
                        pair_copy(copy, t, k).then_inc(late_act, 1)
                if t:
                    h2_relu(t - 1)
                    act.wait_ge(late_full, LATE_FILL["l1", t - 1] + 1)
                n = LATE_FILL["turn", t]
                act.wait_ge(late_full, n + 1)
                for k in range(KT):
                    last = copy(pT_hi[:, k, :].rearrange("p (q j) -> p j q", j=QUADS),
                                late[:, n % 2, k * P:(k + 1) * P].rearrange("p (j q) -> p j q", j=QUADS))
                last.then_inc(pT_hi_ready, 1)
            h1_split(TILES - 1)
            h2_relu(TILES - 1)

        @block.vector
        def _(dve):
            copy = dve.tensor_copy

            def split_lo(i):
                c = CHUNKS[i]
                dve.wait_ge(hi_ready, i + 1)
                if i >= 2:
                    dve.wait_ge(look_full, table_fill(i - 2) + 1)
                dve.tensor_tensor(table_lo[0:KP, i % 2, 0:c, :], table[0:KP, i % 2, 0:c, :],
                                  table_hi[0:KP, i % 2, 0:c, :].bitcast(F32), ALU.subtract).then_inc(lo_ready, 1)

            def one_hot(i):
                dve.wait_ge(ids_in[i % IDS_RING], 16 * (i // IDS_RING + 1))
                for c in range(CHUNKS[i]):
                    n = CHUNK0[i] + c
                    if n >= OH_RING:
                        free = n - OH_RING
                        k = max(a for a in range(NOH) if CHUNK0[a] <= free)
                        if free == CHUNK0[k + 1] - 1:
                            dve.wait_ge(look_full, table_fill(k) + 1)
                        else:
                            dve.wait_ge(onehot_used, free + 1 - k)
                    dve.tensor_scalar(onehot[0:KP, n % OH_RING, :], ids[0:KP, i % IDS_RING, :],
                                      row0[CHUNKS[i]][0:KP, c:c + 1], None, ALU.is_equal
                                      ).then_inc(onehot_ready, 1)

            dve.memset(eT[:, :, NF:SLOTS], 0.0)
            dve.memset(bias[:, :].bitcast(F32), 0.0)
            dve.memset(ones[:, :].bitcast(F32), 1.0).then_inc(pads_ready, 1)
            dve.wait_ge(row0_ready, len(row0))
            split_lo(0)
            for i in range(NOH):
                one_hot(i)
                if i + 1 < NOH:
                    split_lo(i + 1)
                if i == 0:
                    dve.wait_ge(x_hi_ready, 1)
                    dve.tensor_tensor(x_lo[:, :], look[:, 0, :], x_hi[:, :].bitcast(F32), ALU.subtract
                                      ).then_inc(x_lo_ready, 1)
                if i >= LATE and not group_on_act(0, i - LATE):
                    group_copy(dve, copy, 0, i - LATE, eT_dve)
                if i == LATE + 1:
                    dve.wait_ge(w_in, 16 * 5)
                    dve.tensor_tensor(w1_raw[:, KT, :], w1_raw[:, KT, :], w1_raw[:, KT + 1, :], ALU.add
                                      ).then_inc(w_sum, 1)
            if not group_on_act(0, NGR - 1):
                group_copy(dve, copy, 0, NGR - 1, eT_dve)
            dve.wait_ge(w_hi, 3)
            dve.wait_ge(w_sum, 1)
            dve.tensor_tensor(bias[32:33, :], bias_raw[:, :], bias[0:1, :].bitcast(F32), ALU.subtract
                              ).then_inc(w_lo, 1)
            dve.tensor_tensor(w1_lo[:, :, :], w1_raw[:, 0:K1, :], w1_hi[:, :, :].bitcast(F32), ALU.subtract
                              ).then_inc(w_lo, 1)
            dve.tensor_tensor(w2_lo[:, :, :], w2_raw[:, :, :], w2_hi[:, :, :].bitcast(F32), ALU.subtract
                              ).then_inc(w_lo, 1)

            def h1_rest(t):
                n = LATE_FILL["l1", t]
                dve.wait_ge(h1_hi_ready, t + 1)
                if t:
                    dve.wait_ge(late_full, LATE_FILL["l2", t - 1] + 1)
                dve.scalar_tensor_tensor(out=h1_lo[:, :, :],
                                         in0=late[:, n % 2, :].rearrange("n (k b) -> n k b", k=N1),
                                         scalar=0.0, in1=h1_hi[:, :, :].bitcast(F32),
                                         op0=ALU.max, op1=ALU.subtract).then_inc(late_dve, 1)

            def y_copy(t):
                n = LATE_FILL["l3", t]
                dve.wait_ge(late_full, n + 1)
                copy(y[0:1, t * P:(t + 1) * P], late[0:1, n % 2, 0:P]).then_inc(late_dve, 1)

            for t in range(TILES):
                if t:
                    for g in range(NGR):
                        if not group_on_act(t, g):
                            group_copy(dve, copy, t, g, eT_dve)
                    dve.wait_ge(late_full, LATE_FILL["pair", t - 1, NB2 - 1] + 1)
                for c in range(NCH):
                    dve.wait_ge(gram_full, t * NCH + c + 1)
                    dots_copy(copy, t, c, 2)
                    dots_copy(copy, t, c, 3).then_inc(dots_dve, 1)
                if t:
                    h1_rest(t - 1)
                    dve.wait_ge(late_full, LATE_FILL["turn", t - 1] + 1)
                for k in range(NB2):
                    if not late_on_act(("pair", t, k)):
                        dve.wait_ge(late_full, LATE_FILL["pair", t, k] + 1)
                        pair_copy(copy, t, k).then_inc(late_dve, 1)
                if t:
                    y_copy(t - 1)
                n = LATE_FILL["turn", t]
                dve.wait_ge(pT_hi_ready, t + 1)
                for k in range(KT):
                    part = pT_lo[:, k, :].rearrange("p (q j) -> p j q", j=QUADS)
                    hi = pT_hi[:, k, :].bitcast(F32).rearrange("p (q j) -> p j q", j=QUADS)
                    last = dve.tensor_tensor(part, late[:, n % 2, k * P:(k + 1) * P].rearrange(
                        "p (j q) -> p j q", j=QUADS), hi, ALU.subtract)
                last.then_inc(late_dve, 1)
            h1_rest(TILES - 1)
            y_copy(TILES - 1)


def kernel(**inputs):
    import numpy as np
    import concourse.bacc as bacc
    from concourse.bass_utils import run_bass_kernel_spmd

    ids = np.ascontiguousarray(inputs["ids"])
    w1 = np.ascontiguousarray(inputs["W_top1"])
    npairs = NF * (NF - 1) // 2
    w1_rows = np.zeros((NPAIR + 2 * P, H1), w1.dtype)
    for n, r in enumerate(pair_rows_of_w1()):
        if r is not None:
            w1_rows[n] = w1[r]
    w1_rows[NPAIR:NPAIR + P] = w1[0:P]
    w1_rows[NPAIR + P:] = w1[P + npairs:]
    arrays = {
        "dense": np.ascontiguousarray(inputs["r_dense_features"]),
        "ids_rows": np.ascontiguousarray(ids.reshape(TILES, P, NTAB).transpose(1, 0, 2)),
        "ids_bcast": np.ascontiguousarray(ids.T),
        "w1": np.ascontiguousarray(w1_rows.reshape(K1 + 1, P, H1).transpose(1, 0, 2)),
        "b1": np.ascontiguousarray(inputs["b_top1"]).reshape(1, H1),
        "w2": np.ascontiguousarray(np.asarray(inputs["W_top2"]).reshape(N1, P, H2).transpose(1, 0, 2)),
        "b2": np.ascontiguousarray(inputs["b_top2"]).reshape(1, H2),
        "w3": np.ascontiguousarray(np.asarray(inputs["W_top3"]).reshape(N2, P).T),
    }
    for f in range(NTAB):
        arrays[f"tbl_{f}"] = np.ascontiguousarray(inputs[f"tbl_{f}"])

    nc = bacc.Bacc("TRN2", target_bir_lowering=False, num_devices=1)
    ap = {name: nc.dram_tensor(f"in_{name}", a.shape, mybir.dt.from_np(a.dtype), kind="ExternalInput").ap()
          for name, a in arrays.items()}
    out = nc.dram_tensor("out_y", (1, B), F32, kind="ExternalOutput").ap()
    build(nc, ap["dense"], ap["ids_rows"], ap["ids_bcast"], [ap[f"tbl_{f}"] for f in range(NTAB)],
          ap["w1"], ap["b1"], ap["w2"], ap["b2"], ap["w3"], out)
    r = run_bass_kernel_spmd(nc, [{f"in_{name}": a for name, a in arrays.items()}], core_ids=[0])
    return r.results[0]["out_y"].reshape(B, 1)
```

```python
import concourse.bass as bass
from concourse import mybir
from contextlib import ExitStack

F32 = mybir.dt.float32
F32R = mybir.dt.float32r
I32 = mybir.dt.int32
ACT = mybir.ActivationFunctionType
ALU = mybir.AluOpType

P = 128
B = 512
TILES = B // P
ROWS = [12500, 1000, 1250, 12500, 125000, 1250, 12500, 12500, 1250, 1000, 1000, 1000, 1250,
        1250, 1250, 1000, 1250, 12500, 1250, 1250, 1250, 1000, 1000, 1250, 1250, 1000]
NTAB = len(ROWS)
NF = NTAB + 1
SLOTS = 32

ONE_HOT = [1, 9, 10, 11, 15, 21]
GATHERED = [f for f in range(NTAB) if f not in ONE_HOT]
KP = 125
CHUNKS = [ROWS[f] // KP for f in ONE_HOT]
MAXC = max(CHUNKS)
CHUNK0 = [sum(CHUNKS[:i]) for i in range(len(ONE_HOT) + 1)]
NOH, NG = len(ONE_HOT), len(GATHERED)
SLOT_FEATURE = [0] + [f + 1 for f in GATHERED] + [f + 1 for f in ONE_HOT]

GROUP = 4
GROUPS = [list(range(a, min(a + GROUP, NG))) for a in range(0, NG, GROUP)]
NGR = len(GROUPS)

NG_COL = NF - 1
QUADS = P // 32
Q = P // QUADS
CHUNK_Q = 8
NCH = Q // CHUNK_Q
BLOCKS = [(0, 4), (4, 4), (8, 4), (12, 4), (16, 4), (20, 2), (22, 2), (24, 1), (25, 1)]
BLOCK_OFF = [sum(n * (NF - 1 - g) for g, n in BLOCKS[:i]) for i in range(len(BLOCKS) + 1)]
NPAIR = BLOCK_OFF[-1] + 1
KT = NPAIR // P
assert KT * P == NPAIR
BANKS2 = [[0], [1], [2], [3], [4], [5, 6], [7, 8]]
NB2 = len(BANKS2)
HALVES, HB, HQ = 2, B // 2, 2 * Q
H1, H2 = 512, 256
N1, N2 = H1 // P, H2 // P
K1 = KT + 1

OH_RING, IDS_RING = 8, 4


def pair_rows_of_w1():
    rows = []
    for g0, n in BLOCKS:
        for g in range(g0, g0 + n):
            for f in range(g0 + 1, NF):
                if f <= g:
                    rows.append(None)
                    continue
                i, j = sorted((SLOT_FEATURE[g], SLOT_FEATURE[f]))
                rows.append(P + i * NF - i * (i + 1) // 2 + (j - i - 1))
    return rows


ACT_CHUNK = [(i, c) for i in range(NOH) for c in (3, 7)]
DVE_CHUNK = [(i, c) for i in range(NOH) for c in range(CHUNKS[i]) if (i, c) not in ACT_CHUNK]


def chunks_made(chunks, i):
    return len([k for k in chunks if k[0] <= i])


ALL_GROUPS = [(t, g) for t in range(TILES) for g in range(NGR)]
FIRST_TABLE = 1
EARLY = ALL_GROUPS[:NOH - FIRST_TABLE]
REST = {t: [(t, g) for g in range(NGR) if (t, g) not in EARLY] for t in range(TILES)}
LOOK_ORDER = [("dense",)]
for _i in range(NOH):
    LOOK_ORDER.append(("table", _i))
    if _i >= FIRST_TABLE:
        LOOK_ORDER.append(("group", *EARLY[_i - FIRST_TABLE]))
for _t in (0, 1):
    LOOK_ORDER += [("group", *k) for k in REST[_t]]
SPREAD = REST[2][:2]
LOOK_ORDER += [("group", *k) for k in SPREAD]
LOOK_ORDER += [("layer1", 0, 0), ("layer1", 0, 1)]
LOOK_ORDER += [("group", *k) for k in REST[2][2:] + REST[3]]
LOOK_ORDER += [("layer1", 1, 0), ("layer1", 1, 1)]
LOOK = {what: n for n, what in enumerate(LOOK_ORDER)}


def look_on_act(what):
    return what[0] == "table" or (what[0] == "group" and what[2] % 2 == 1)


LOOK_ACT = [w for w in LOOK_ORDER if look_on_act(w)]
LOOK_DVE = [w for w in LOOK_ORDER if not look_on_act(w)]

LATE_ORDER = []
for _h in range(HALVES):
    LATE_ORDER += [("pair", _h, k) for k in range(NB2)]
    LATE_ORDER += [("turn", _h, 0), ("turn", _h, 1), ("layer2", _h), ("layer3", _h)]
LATE = {what: n for n, what in enumerate(LATE_ORDER)}
TURNED = [[0, 1], [2]]


def late_on_act(what):
    return what[0] == "layer2" or (what[0] == "pair" and what[2] % 2 == 0)


LATE_ACT = [w for w in LATE_ORDER if late_on_act(w)]
LATE_DVE = [w for w in LATE_ORDER if not late_on_act(w)]


def build(nc, dense, ids_rows, ids_bcast, tables, w1, w2, b2, w3, out):
    with ExitStack() as ctx:
        def sb(name, shape, dt=F32):
            return ctx.enter_context(nc.sbuf_tensor(name, shape, dt))

        def sem(name):
            return ctx.enter_context(nc.semaphore(name))

        idx = sb("idx", [P, TILES, NTAB], I32)
        ids = sb("ids", [P, IDS_RING, B], I32)
        row0 = {c: sb(f"row_of_partition_{c}", [P, c]) for c in sorted(set(CHUNKS))}
        x_rows = sb("x_rows", [P, TILES, P])
        e_rows = sb("e_rows", [P, 2, NG, P])
        table = sb("table", [P, 2, MAXC, P])
        table_hi = sb("table_hi", [P, 2, MAXC, P], F32R)
        table_lo = sb("table_lo", [P, 2, MAXC, P], F32R)
        onehot = sb("onehot", [P, OH_RING, B], F32R)
        distance = sb("distance", [P, 2, B])
        eT = sb("eT", [P, B, SLOTS])
        x_hi = sb("x_hi", [P, B], F32R)
        x_lo = sb("x_lo", [P, B], F32R)
        dots = sb("dots", [P, NG_COL, HQ])
        pair_rows = sb("pair_rows", [HQ, QUADS, NPAIR])
        pT_hi = sb("pT_hi", [P, KT, HB], F32R)
        pT_lo = sb("pT_lo", [P, KT, HB], F32R)
        w1_raw = sb("w1_raw", [P, K1 + 1, H1])
        w1_hi = sb("w1_hi", [P, K1, H1], F32R)
        w1_lo = sb("w1_lo", [P, K1, H1], F32R)
        w2_raw = sb("w2_raw", [P, N1, H2])
        w2_hi = sb("w2_hi", [P, N1, H2], F32R)
        w2_lo = sb("w2_lo", [P, N1, H2], F32R)
        w3_sb = sb("w3_sb", [P, N2])
        b2_sb = sb("b2_sb", [P, N2])
        h1_hi = onehot[:, 0:2, :].rearrange("p a (k b) -> p (a k) b", b=HB)
        h1_lo = onehot[:, 2:4, :].rearrange("p a (k b) -> p (a k) b", b=HB)
        h2 = sb("h2", [P, N2, HB])
        y = sb("y", [1, B])
        ident = sb("ident", [P, P])
        one_col = sb("one_col", [P, P])
        zero = sb("zero", [P, 1])

        look = ctx.enter_context(nc.psum_tensor("look", [P, 2, B], F32))
        gram = ctx.enter_context(nc.psum_tensor("gram", [P, 2, CHUNK_Q, P], F32))
        late = ctx.enter_context(nc.psum_tensor("late", [P, 2, B], F32))

        idx_in = sem("idx_in")
        ids_in = [sem(f"ids_in{k}") for k in range(IDS_RING)]
        table_in = [sem(f"table_in{k}") for k in range(2)]
        x_in = sem("x_in")
        w_in = sem("w_in")
        rows_in = [[sem(f"rows_in{t}_{g}") for g in range(NGR)] for t in range(TILES)]
        y_out = sem("y_out")
        ident_ready = sem("ident_ready")
        row0_ready = sem("row0_ready")
        zero_ready = sem("zero_ready")
        pads_ready = sem("pads_ready")
        bias_one = sem("bias_one")
        hi_ready = sem("hi_ready")
        lo_ready = sem("lo_ready")
        distance_ready = sem("distance_ready")
        onehot_act = sem("onehot_act")
        onehot_dve = sem("onehot_dve")
        onehot_used = sem("onehot_used")
        look_full = sem("look_full")
        look_act = sem("look_act")
        look_dve = sem("look_dve")
        x_hi_ready = sem("x_hi_ready")
        w_sum = sem("w_sum")
        w_hi = sem("w_hi")
        w_lo = sem("w_lo")
        gram_full = sem("gram_full")
        dots_act = sem("dots_act")
        dots_dve = sem("dots_dve")
        late_full = sem("late_full")
        late_act = sem("late_act")
        late_dve = sem("late_dve")
        pT_hi_ready = sem("pT_hi_ready")
        h1_hi_ready = sem("h1_hi_ready")

        block = ctx.enter_context(nc.Block())

        def wait_look_done(eng, what):
            if look_on_act(what):
                eng.wait_ge(look_act, LOOK_ACT.index(what) + 1)
            else:
                eng.wait_ge(look_dve, LOOK_DVE.index(what) + 1)

        def wait_look_full(eng, what):
            eng.wait_ge(look_full, LOOK[what] + 1)

        def wait_late_done(eng, what):
            if late_on_act(what):
                eng.wait_ge(late_act, LATE_ACT.index(what) + 1)
            else:
                eng.wait_ge(late_dve, LATE_DVE.index(what) + 1)

        def wait_late_full(eng, what):
            eng.wait_ge(late_full, LATE[what] + 1)

        def wait_onehot_free(eng, free):
            if free < 0:
                return
            k = max(a for a in range(NOH) if CHUNK0[a] <= free)
            if free == CHUNK0[k + 1] - 1:
                wait_look_full(eng, ("table", k))
            else:
                eng.wait_ge(onehot_used, free + 1 - k)

        @block.sync
        def _(sp):
            def load_table(i):
                c = CHUNKS[i]
                if i >= 2:
                    sp.wait_ge(lo_ready, i - 1)
                sp.dma_start(table[0:KP, i % 2, 0:c, :],
                             tables[ONE_HOT[i]].rearrange("(p c) d -> p c d", c=c)).then_inc(table_in[i % 2], 16)

            def load_ids(i):
                if i >= IDS_RING:
                    sp.wait_ge(onehot_dve, chunks_made(DVE_CHUNK, i - IDS_RING))
                    sp.wait_ge(onehot_act, chunks_made(ACT_CHUNK, i - IDS_RING))
                sp.dma_start(ids[:, i % IDS_RING, :], ids_bcast[ONE_HOT[i]:ONE_HOT[i] + 1, :].to_broadcast([P, B])
                             ).then_inc(ids_in[i % IDS_RING], 16)

            sp.dma_start(idx[:, :, :], ids_rows).then_inc(idx_in, 16)
            load_table(0)
            load_ids(1)
            load_table(1)
            sp.dma_start(x_rows[:, :, :], dense.rearrange("(t p) d -> p t d", p=P)).then_inc(x_in, 16)
            load_ids(2)
            load_ids(3)
            for i in range(2, NOH):
                load_table(i)
                if i + 2 < NOH:
                    load_ids(i + 2)
                if i == 3:
                    sp.dma_start(w1_raw[:, :, :], w1).then_inc(w_in, 16)
                    sp.dma_start(w2_raw[:, :, :], w2).then_inc(w_in, 16)
                    sp.dma_start(b2_sb[:, :], b2).then_inc(w_in, 16)
                    sp.dma_start(w3_sb[:, :], w3).then_inc(w_in, 16)
            wait_late_done(sp, ("layer3", HALVES - 1))
            sp.dma_start(out, y[:, :]).then_inc(y_out, 16)
            sp.wait_ge(y_out, 16)

        @block.gpsimd
        def _(pool):
            pool.memset(zero[:, :], 0.0).then_inc(zero_ready, 1)
            for c in sorted(row0):
                pool.iota(row0[c][:, :], pattern=[[1, c]], base=0, channel_multiplier=c,
                          allow_small_or_imprecise_dtypes=True).then_inc(row0_ready, 1)
            pool.memset(one_col[:, :], 1.0).then_inc(ident_ready, 1)
            pool.wait_ge(ident_ready, 1)
            pool.affine_select(out=ident[:, :], in_=one_col[:, :], compare_op=ALU.is_equal, fill=0.0,
                               base=0, pattern=[[-1, P]], channel_multiplier=1).then_inc(ident_ready, 1)
            pool.memset(pair_rows[:, :, NPAIR - 1:NPAIR], 1.0).then_inc(bias_one, 1)
            pool.wait_ge(idx_in, 16)
            for t, g in ALL_GROUPS:
                if t >= 2:
                    wait_look_full(pool, ("group", t - 2, g))
                for s in GROUPS[g]:
                    f = GATHERED[s]
                    pool.indirect_dma_start(
                        out=e_rows[:, t % 2, s, :], out_offset=None, in_=tables[f][:, :],
                        in_offset=bass.IndirectOffsetOnAxis(ap=idx[:, t, f:f + 1], axis=0)
                    ).then_inc(rows_in[t][g], 16)

        @block.tensor
        def _(pe):
            def look_bank(what):
                n = LOOK[what]
                if n >= 2:
                    wait_look_done(pe, LOOK_ORDER[n - 2])
                return look[:, n % 2, :]

            def late_bank(what):
                n = LATE[what]
                if n >= 2:
                    wait_late_done(pe, LATE_ORDER[n - 2])
                return late[:, n % 2, :]

            def turn_dense():
                pe.wait_ge(ident_ready, 2)
                pe.wait_ge(x_in, 16)
                bank = look_bank(("dense",))
                for t in range(TILES):
                    last = pe.transpose(bank[:, t * P:(t + 1) * P], x_rows[:, t, :], ident[:, :])
                last.then_inc(look_full, 1)

            def one_hot_product(i):
                bank = look_bank(("table", i))
                pe.wait_ge(hi_ready, i + 1)
                pe.wait_ge(lo_ready, i + 1)
                for c in range(CHUNKS[i]):
                    if (i, c) in ACT_CHUNK:
                        pe.wait_ge(onehot_act, ACT_CHUNK.index((i, c)) + 1)
                    else:
                        pe.wait_ge(onehot_dve, DVE_CHUNK.index((i, c)) + 1)
                    hot = onehot[0:KP, (CHUNK0[i] + c) % OH_RING, :]
                    pe.matmul(bank, table_hi[0:KP, i % 2, c, :], hot, start=c == 0, stop=False)
                    last = pe.matmul(bank, table_lo[0:KP, i % 2, c, :], hot, start=False, stop=c == CHUNKS[i] - 1)
                    if c < CHUNKS[i] - 1:
                        last.then_inc(onehot_used, 1)
                last.then_inc(look_full, 1)

            def turn_group(t, g):
                bank = look_bank(("group", t, g))
                pe.wait_ge(rows_in[t][g], 16 * len(GROUPS[g]))
                for k, s in enumerate(GROUPS[g]):
                    last = pe.transpose(bank[:, k * P:(k + 1) * P], e_rows[:, t % 2, s, :], ident[:, :])
                last.then_inc(look_full, 1)

            def gram_tile(t):
                upto = LOOK["group", t, NGR - 1]
                if t == 0:
                    upto = max(upto, LOOK["table", NOH - 1])
                    pe.wait_ge(pads_ready, 1)
                pe.wait_ge(look_act, len([w for w in LOOK_ACT if LOOK[w] <= upto]))
                pe.wait_ge(look_dve, len([w for w in LOOK_DVE if LOOK[w] <= upto]))
                for c in range(NCH):
                    n = t * NCH + c
                    if n >= 2:
                        pe.wait_ge(dots_act, n - 1)
                        pe.wait_ge(dots_dve, n - 1)
                    for q in range(CHUNK_Q):
                        b = t * P + (c * CHUNK_Q + q) * QUADS
                        last = pe.matmul(gram[:, n % 2, q, 0:QUADS * NG_COL], eT[:, b:b + QUADS, :],
                                         eT[:, b:b + QUADS, 0:NG_COL], start=True, stop=True)
                    last.then_inc(gram_full, 1)

            def pairs_half(h):
                pe.wait_ge(dots_act, 2 * (h + 1) * NCH)
                pe.wait_ge(dots_dve, 2 * (h + 1) * NCH)
                for k, blocks in enumerate(BANKS2):
                    bank = late_bank(("pair", h, k))
                    g0, g1 = BLOCKS[blocks[0]][0], sum(BLOCKS[blocks[-1]])
                    for g in range(g0, g1):
                        last = pe.transpose(bank[0:HQ, (g - g0) * P:(g - g0 + 1) * P], dots[:, g, :], ident[:, :])
                    last.then_inc(late_full, 1)

            def turn_pairs(h):
                for i, ks in enumerate(TURNED):
                    bank = late_bank(("turn", h, i))
                    if i == 0:
                        pe.wait_ge(bias_one, 1)
                        for k in range(NB2):
                            wait_late_done(pe, ("pair", h, k))
                    for m, k in enumerate(ks):
                        for j in range(QUADS):
                            at = m * HB + j * HQ
                            last = pe.transpose(bank[:, at:at + HQ], pair_rows[:, j, k * P:(k + 1) * P],
                                                ident[0:HQ, 0:HQ])
                    last.then_inc(late_full, 1)

            def layer1_tile(bank, n, k, hi, lo, first, last_one):
                o = bank[:, (n % 2) * HB:(n % 2 + 1) * HB]
                rows = slice(n * P, (n + 1) * P)
                pe.matmul(o, w1_hi[:, k, rows], hi, start=first, stop=False, skip_group_check=True)
                pe.matmul(o, w1_hi[:, k, rows], lo, start=False, stop=False, skip_group_check=True)
                return pe.matmul(o, w1_lo[:, k, rows], hi, start=False, stop=last_one, skip_group_check=True)

            def layer1_dense(h):
                if h == 0:
                    pe.wait_ge(w_hi, 1)
                    pe.wait_ge(w_lo, 1)
                cols = slice(h * HB, (h + 1) * HB)
                for i in range(2):
                    bank = look_bank(("layer1", h, i))
                    for n in (2 * i, 2 * i + 1):
                        layer1_tile(bank, n, KT, x_hi[:, cols], x_lo[:, cols], n % 2 == 0, False)

            def layer1_pairs(h):
                for i in range(2):
                    bank = look[:, LOOK["layer1", h, i] % 2, :]
                    for n in (2 * i, 2 * i + 1):
                        for k in range(KT):
                            if n == 0 and k in (0, 2):
                                wait_late_done(pe, ("turn", h, k // 2))
                            last = layer1_tile(bank, n, k, pT_hi[:, k, :], pT_lo[:, k, :], False, k == KT - 1)
                    last.then_inc(look_full, 1)

            def layer2(h):
                bank = late_bank(("layer2", h))
                if h == 0:
                    pe.wait_ge(w_hi, 2)
                    pe.wait_ge(w_lo, 2)
                for k in range(N1):
                    if k % 2 == 0:
                        wait_look_done(pe, ("layer1", h, k // 2))
                    for n in range(N2):
                        o = bank[:, n * HB:(n + 1) * HB]
                        rows = slice(n * P, (n + 1) * P)
                        end = k == N1 - 1
                        pe.matmul(o, w2_hi[:, k, rows], h1_hi[:, k, :], start=k == 0 and n == 0, stop=False,
                                  skip_group_check=True)
                        pe.matmul(o, w2_hi[:, k, rows], h1_lo[:, k, :], start=False, stop=False,
                                  skip_group_check=True)
                        last = pe.matmul(o, w2_lo[:, k, rows], h1_hi[:, k, :], start=False, stop=end,
                                         skip_group_check=True)
                last.then_inc(late_full, 1)

            def layer3(h):
                bank = late_bank(("layer3", h))
                wait_late_done(pe, ("layer2", h))
                for k in range(N2):
                    last = pe.matmul(bank[0:1, 0:HB], w3_sb[:, k:k + 1], h2[:, k, :], start=k == 0, stop=k == N2 - 1)
                last.then_inc(late_full, 1)

            turn_dense()
            for i in range(NOH):
                one_hot_product(i)
                if i >= FIRST_TABLE:
                    turn_group(*EARLY[i - FIRST_TABLE])
            for k in REST[0]:
                turn_group(*k)
            gram_tile(0)
            for k in REST[1]:
                turn_group(*k)
            gram_tile(1)
            turn_group(*SPREAD[0])
            pairs_half(0)
            turn_group(*SPREAD[1])
            layer1_dense(0)
            turn_pairs(0)
            layer1_pairs(0)
            turn_group(*REST[2][2])
            layer2(0)
            turn_group(*REST[2][3])
            layer3(0)
            for k in REST[2][4:]:
                turn_group(*k)
            gram_tile(2)
            for k in REST[3]:
                turn_group(*k)
            gram_tile(3)
            layer1_dense(1)
            pairs_half(1)
            turn_pairs(1)
            layer1_pairs(1)
            layer2(1)
            layer3(1)

        def group_copy(eng, copy, t, g, done):
            what = ("group", t, g)
            n = len(GROUPS[g])
            wait_look_full(eng, what)
            s = 1 + GROUPS[g][0]
            copy(eT[:, t * P:(t + 1) * P, s:s + n].rearrange("d b f -> d f b"),
                 look[:, LOOK[what] % 2, 0:n * P].rearrange("d (f b) -> d f b", f=n)).then_inc(done, 1)

        def dots_copy(copy, t, c, j):
            n = t * NCH + c
            rows = slice(32 * j, 32 * j + 32)
            q0 = (t % 2) * Q + c * CHUNK_Q
            return copy(dots[rows, :, q0:q0 + CHUNK_Q].rearrange("f g q -> f q g"),
                        gram[rows, n % 2, :, j * NG_COL:(j + 1) * NG_COL])

        def pair_copy(copy, h, k):
            n = LATE["pair", h, k]
            first = BLOCKS[BANKS2[k][0]][0]
            for blk in BANKS2[k]:
                g0, ng = BLOCKS[blk]
                src = late[0:HQ, n % 2, (g0 - first) * P:(g0 - first + ng) * P].rearrange(
                    "q (g j f) -> q g j f", g=ng, j=QUADS)[:, :, :, g0 + 1:NF]
                dst = pair_rows[:, :, BLOCK_OFF[blk]:BLOCK_OFF[blk + 1]].rearrange(
                    "q j (g w) -> q g j w", g=ng)
                last = copy(dst, src)
            return last

        def turned(h, i):
            ks = TURNED[i]
            src = late[:, LATE["turn", h, i] % 2, 0:len(ks) * HB].rearrange(
                "p (k j q) -> p k j q", k=len(ks), j=QUADS)
            return [src] + [t[:, ks[0]:ks[-1] + 1, :].rearrange("p k (q j) -> p k j q", j=QUADS)
                            for t in (pT_hi, pT_lo)]

        @block.scalar
        def _(act):
            def copy(dst, src):
                return act.activation(dst, src, ACT.Copy)

            def split_hi(i):
                act.wait_ge(table_in[i % 2], 16 * (i // 2 + 1))
                if i >= 2:
                    wait_look_full(act, ("table", i - 2))
                c = CHUNKS[i]
                copy(table_hi[0:KP, i % 2, 0:c, :], table[0:KP, i % 2, 0:c, :]).then_inc(hi_ready, 1)

            def one_hot(i, c):
                n = ACT_CHUNK.index((i, c))
                free = CHUNK0[i] + c - OH_RING
                act.activation(distance[0:KP, n % 2, :], ids[0:KP, i % IDS_RING, :], ACT.Abs,
                               bias=row0[CHUNKS[i]][0:KP, c:c + 1], scale=-1.0).then_inc(distance_ready, 1)
                wait_onehot_free(act, free)
                act.wait_ge(distance_ready, n + 1)
                act.activation(onehot[0:KP, (free + OH_RING) % OH_RING, :], distance[0:KP, n % 2, :], ACT.Relu,
                               bias=1.0, scale=-1.0).then_inc(onehot_act, 1)

            def table_copy(i):
                wait_look_full(act, ("table", i))
                copy(eT[:, :, 1 + NG + i], look[:, LOOK["table", i] % 2, :]).then_inc(look_act, 1)

            load_first_ids = act.dma_start(ids[:, 0, :], ids_bcast[ONE_HOT[0]:ONE_HOT[0] + 1, :].to_broadcast([P, B]))
            load_first_ids.then_inc(ids_in[0], 16)
            act.wait_ge(zero_ready, 1)
            copy(eT[:, :, NF:SLOTS], zero[:, :].unsqueeze(2).to_broadcast([P, B, SLOTS - NF])).then_inc(pads_ready, 1)
            act.wait_ge(row0_ready, len(row0))
            split_hi(0)
            for i in range(NOH):
                act.wait_ge(ids_in[i % IDS_RING], 16 * (i // IDS_RING + 1))
                for c in [c for a, c in ACT_CHUNK if a == i]:
                    one_hot(i, c)
                if i == 0:
                    split_hi(1)
                    wait_look_full(act, ("dense",))
                    copy(eT[:, :, 0], look[:, 0, :])
                    copy(x_hi[:, :], look[:, 0, :]).then_inc(x_hi_ready, 1)
                else:
                    table_copy(i - 1)
                    if i + 1 < NOH:
                        split_hi(i + 1)
                if i - 1 >= FIRST_TABLE and look_on_act(("group", *EARLY[i - 1 - FIRST_TABLE])):
                    group_copy(act, copy, *EARLY[i - 1 - FIRST_TABLE], look_act)
                if i == NOH - 1:
                    act.wait_ge(w_in, 16 * 4)
                    act.wait_ge(w_sum, 1)
                    copy(w1_hi[:, :, :], w1_raw[:, 0:K1, :]).then_inc(w_hi, 1)
                    copy(w2_hi[:, :, :], w2_raw[:, :, :]).then_inc(w_hi, 1)
            table_copy(NOH - 1)
            for k in [EARLY[-1]] + REST[0]:
                if look_on_act(("group", *k)):
                    group_copy(act, copy, *k, look_act)

            def groups(ks):
                for k in ks:
                    if look_on_act(("group", *k)):
                        group_copy(act, copy, *k, look_act)

            def dots_tile(t):
                if t == 2:
                    wait_late_full(act, ("pair", 0, NB2 - 1))
                for c in range(NCH):
                    act.wait_ge(gram_full, t * NCH + c + 1)
                    dots_copy(copy, t, c, 0)
                    dots_copy(copy, t, c, 1).then_inc(dots_act, 1)

            def pairs_half(h):
                if h:
                    wait_late_full(act, ("turn", h - 1, 1))
                for k in range(NB2):
                    if late_on_act(("pair", h, k)):
                        wait_late_full(act, ("pair", h, k))
                        pair_copy(copy, h, k).then_inc(late_act, 1)

            def turn_hi(h):
                if h:
                    wait_look_full(act, ("layer1", h - 1, 1))
                for i in range(2):
                    wait_late_full(act, ("turn", h, i))
                    src, hi, _ = turned(h, i)
                    copy(hi, src).then_inc(pT_hi_ready, 1)

            def h1_split(h):
                if h:
                    wait_late_full(act, ("layer2", h - 1))
                for i in range(2):
                    wait_look_full(act, ("layer1", h, i))
                    act.activation(h1_hi[:, 2 * i:2 * i + 2, :], look[:, LOOK["layer1", h, i] % 2, :].rearrange(
                        "n (k b) -> n k b", k=2), ACT.Relu).then_inc(h1_hi_ready, 1)

            def h2_relu(h):
                wait_late_full(act, ("layer2", h))
                if h:
                    wait_late_full(act, ("layer3", h - 1))
                for n in range(N2):
                    last = act.activation(h2[:, n, :], late[:, LATE["layer2", h] % 2, n * HB:(n + 1) * HB],
                                          ACT.Relu, bias=b2_sb[:, n:n + 1])
                last.then_inc(late_act, 1)

            dots_tile(0)
            groups(REST[1])
            dots_tile(1)
            groups(SPREAD[:1])
            pairs_half(0)
            groups(SPREAD[1:])
            turn_hi(0)
            h1_split(0)
            groups(REST[2][2:3])
            h2_relu(0)
            groups(REST[2][3:])
            dots_tile(2)
            groups(REST[3])
            dots_tile(3)
            pairs_half(1)
            turn_hi(1)
            h1_split(1)
            h2_relu(1)

        @block.vector
        def _(dve):
            copy = dve.tensor_copy

            def split_lo(i):
                c = CHUNKS[i]
                dve.wait_ge(hi_ready, i + 1)
                dve.tensor_tensor(table_lo[0:KP, i % 2, 0:c, :], table[0:KP, i % 2, 0:c, :],
                                  table_hi[0:KP, i % 2, 0:c, :].bitcast(F32), ALU.subtract).then_inc(lo_ready, 1)

            def one_hot(i, c):
                n = CHUNK0[i] + c
                wait_onehot_free(dve, n - OH_RING)
                dve.tensor_scalar(onehot[0:KP, n % OH_RING, :], ids[0:KP, i % IDS_RING, :],
                                  row0[CHUNKS[i]][0:KP, c:c + 1], None, ALU.is_equal).then_inc(onehot_dve, 1)

            dve.wait_ge(row0_ready, len(row0))
            for i in range(NOH):
                dve.wait_ge(ids_in[i % IDS_RING], 16 * (i // IDS_RING + 1))
                mine = [c for a, c in DVE_CHUNK if a == i]
                for c in mine[:3]:
                    one_hot(i, c)
                if i == 0:
                    split_lo(0)
                for c in mine[3:]:
                    one_hot(i, c)
                if i == 0:
                    dve.wait_ge(x_hi_ready, 1)
                    dve.tensor_tensor(x_lo[:, :], look[:, 0, :], x_hi[:, :].bitcast(F32), ALU.subtract
                                      ).then_inc(look_dve, 1)
                if i + 1 < NOH:
                    split_lo(i + 1)
                if i - 1 >= FIRST_TABLE and not look_on_act(("group", *EARLY[i - 1 - FIRST_TABLE])):
                    group_copy(dve, copy, *EARLY[i - 1 - FIRST_TABLE], look_dve)
                if i == NOH - 2:
                    dve.wait_ge(w_in, 16 * 4)
                    dve.tensor_tensor(w1_raw[:, KT, :], w1_raw[:, KT, :], w1_raw[:, KT + 1, :], ALU.add
                                      ).then_inc(w_sum, 1)

            def groups(ks):
                for k in ks:
                    if not look_on_act(("group", *k)):
                        group_copy(dve, copy, *k, look_dve)

            def dots_tile(t):
                if t == 2:
                    wait_late_full(dve, ("pair", 0, NB2 - 1))
                for c in range(NCH):
                    dve.wait_ge(gram_full, t * NCH + c + 1)
                    dots_copy(copy, t, c, 2)
                    dots_copy(copy, t, c, 3).then_inc(dots_dve, 1)

            def pairs_half(h):
                if h:
                    wait_late_full(dve, ("turn", h - 1, 1))
                for k in range(NB2):
                    if not late_on_act(("pair", h, k)):
                        wait_late_full(dve, ("pair", h, k))
                        pair_copy(copy, h, k).then_inc(late_dve, 1)

            def turn_lo(h):
                for i in range(2):
                    dve.wait_ge(pT_hi_ready, 2 * h + i + 1)
                    src, hi, lo = turned(h, i)
                    for k in range(len(TURNED[i])):
                        last = dve.tensor_tensor(lo[:, k], src[:, k], hi[:, k].bitcast(F32), ALU.subtract)
                    last.then_inc(late_dve, 1)

            def h1_rest(h):
                for i in range(2):
                    dve.wait_ge(h1_hi_ready, 2 * h + i + 1)
                    rows = slice(2 * i, 2 * i + 2)
                    dve.scalar_tensor_tensor(out=h1_lo[:, rows, :],
                                             in0=look[:, LOOK["layer1", h, i] % 2, :].rearrange(
                                                 "n (k b) -> n k b", k=2),
                                             scalar=0.0, in1=h1_hi[:, rows, :].bitcast(F32),
                                             op0=ALU.max, op1=ALU.subtract).then_inc(look_dve, 1)

            def y_copy(h):
                wait_late_full(dve, ("layer3", h))
                copy(y[0:1, h * HB:(h + 1) * HB], late[0:1, LATE["layer3", h] % 2, 0:HB]).then_inc(late_dve, 1)

            groups([EARLY[-1]] + REST[0])
            dots_tile(0)
            groups(REST[1])
            dve.wait_ge(w_hi, 1)
            dve.tensor_tensor(w1_lo[:, :, :], w1_raw[:, 0:K1, :], w1_hi[:, :, :].bitcast(F32), ALU.subtract
                              ).then_inc(w_lo, 1)
            dots_tile(1)
            groups(SPREAD[:1])
            pairs_half(0)
            groups(SPREAD[1:])
            turn_lo(0)
            dve.wait_ge(w_hi, 2)
            dve.tensor_tensor(w2_lo[:, :, :], w2_raw[:, :, :], w2_hi[:, :, :].bitcast(F32), ALU.subtract
                              ).then_inc(w_lo, 1)
            h1_rest(0)
            groups(REST[2][2:4])
            y_copy(0)
            groups(REST[2][4:])
            dots_tile(2)
            groups(REST[3])
            dots_tile(3)
            pairs_half(1)
            turn_lo(1)
            h1_rest(1)
            y_copy(1)


def kernel(**inputs):
    import numpy as np
    import concourse.bacc as bacc
    from concourse.bass_utils import run_bass_kernel_spmd

    ids = np.ascontiguousarray(inputs["ids"])
    w1 = np.ascontiguousarray(inputs["W_top1"])
    npairs = NF * (NF - 1) // 2
    w1_rows = np.zeros((NPAIR + 2 * P, H1), w1.dtype)
    w1_rows[NPAIR - 1] = inputs["b_top1"]
    for n, r in enumerate(pair_rows_of_w1()):
        if r is not None:
            w1_rows[n] = w1[r]
    w1_rows[NPAIR:NPAIR + P] = w1[0:P]
    w1_rows[NPAIR + P:] = w1[P + npairs:]
    arrays = {
        "dense": np.ascontiguousarray(inputs["r_dense_features"]),
        "ids_rows": np.ascontiguousarray(ids.reshape(TILES, P, NTAB).transpose(1, 0, 2)),
        "ids_bcast": np.ascontiguousarray(ids.T),
        "w1": np.ascontiguousarray(w1_rows.reshape(K1 + 1, P, H1).transpose(1, 0, 2)),
        "w2": np.ascontiguousarray(np.asarray(inputs["W_top2"]).reshape(N1, P, H2).transpose(1, 0, 2)),
        "b2": np.ascontiguousarray(np.asarray(inputs["b_top2"]).reshape(N2, P).T),
        "w3": np.ascontiguousarray(np.asarray(inputs["W_top3"]).reshape(N2, P).T),
    }
    for f in range(NTAB):
        arrays[f"tbl_{f}"] = np.ascontiguousarray(inputs[f"tbl_{f}"])

    nc = bacc.Bacc("TRN2", target_bir_lowering=False, num_devices=1)
    ap = {name: nc.dram_tensor(f"in_{name}", a.shape, mybir.dt.from_np(a.dtype), kind="ExternalInput").ap()
          for name, a in arrays.items()}
    out = nc.dram_tensor("out_y", (1, B), F32, kind="ExternalOutput").ap()
    build(nc, ap["dense"], ap["ids_rows"], ap["ids_bcast"], [ap[f"tbl_{f}"] for f in range(NTAB)],
          ap["w1"], ap["w2"], ap["b2"], ap["w3"], out)
    r = run_bass_kernel_spmd(nc, [{f"in_{name}": a for name, a in arrays.items()}], core_ids=[0])
    return r.results[0]["out_y"].reshape(B, 1)
```

```python
import concourse.bass as bass
from concourse import mybir
from contextlib import ExitStack

F32 = mybir.dt.float32
F32R = mybir.dt.float32r
I32 = mybir.dt.int32
ACT = mybir.ActivationFunctionType
ALU = mybir.AluOpType

P = 128
B = 512
TILES = B // P
ROWS = [12500, 1000, 1250, 12500, 125000, 1250, 12500, 12500, 1250, 1000, 1000, 1000, 1250,
        1250, 1250, 1000, 1250, 12500, 1250, 1250, 1250, 1000, 1000, 1250, 1250, 1000]
NTAB = len(ROWS)
NF = NTAB + 1
SLOTS = 32

ONE_HOT = [1, 9, 10, 11, 15, 21, 22]
GATHERED = [f for f in range(NTAB) if f not in ONE_HOT]
KP = 125
CHUNKS = [ROWS[f] // KP for f in ONE_HOT]
MAXC = max(CHUNKS)
CHUNK0 = [sum(CHUNKS[:i]) for i in range(len(ONE_HOT) + 1)]
NOH, NG = len(ONE_HOT), len(GATHERED)
SLOT_FEATURE = [0] + [f + 1 for f in GATHERED] + [f + 1 for f in ONE_HOT]

GROUP = 4
GROUPS = [list(range(a, min(a + GROUP, NG))) for a in range(0, NG, GROUP)]
NGR = len(GROUPS)

NG_COL = NF - 1
QUADS = P // 32
Q = P // QUADS
CHUNK_Q = 8
NCH = Q // CHUNK_Q
BLOCKS = [(0, 4), (4, 4), (8, 4), (12, 4), (16, 4), (20, 2), (22, 2), (24, 1), (25, 1)]
BLOCK_OFF = [sum(n * (NF - 1 - g) for g, n in BLOCKS[:i]) for i in range(len(BLOCKS) + 1)]
NPAIR = BLOCK_OFF[-1] + 1
KT = NPAIR // P
assert KT * P == NPAIR
BANKS2 = [[0], [1], [2], [3], [4], [5, 6], [7, 8]]
NB2 = len(BANKS2)
HALVES, HB, HQ = 2, B // 2, 2 * Q
H1, H2 = 512, 256
N1, N2 = H1 // P, H2 // P
K1 = KT + 1

OH_RING, IDS_RING = 8, 4
WARM_UP = 9


def pair_rows_of_w1():
    rows = []
    for g0, n in BLOCKS:
        for g in range(g0, g0 + n):
            for f in range(g0 + 1, NF):
                if f <= g:
                    rows.append(None)
                    continue
                i, j = sorted((SLOT_FEATURE[g], SLOT_FEATURE[f]))
                rows.append(P + i * NF - i * (i + 1) // 2 + (j - i - 1))
    return rows


ACT_CHUNK = [(i, c) for i in range(NOH) for c in (3, 7)]
DVE_CHUNK = [(i, c) for i in range(NOH) for c in range(CHUNKS[i]) if (i, c) not in ACT_CHUNK]


def chunks_made(chunks, i):
    return len([k for k in chunks if k[0] <= i])


PIECES = [[(0, 4), (4, CHUNKS[0])]] + [[(0, c)] for c in CHUNKS[1:]]


def pieces_split(i, c=None):
    return sum(len(p) for p in PIECES[:i]) + len([p for p in PIECES[i] if c is None or p[0] <= c])


ALL_GROUPS = [(t, g) for t in range(TILES) for g in range(NGR)]
FIRST_TABLE = 1
EARLY = ALL_GROUPS[:NOH - FIRST_TABLE]
REST = {t: [(t, g) for g in range(NGR) if (t, g) not in EARLY] for t in range(TILES)}
BESIDE_GRAM = {0: REST[1][:NCH], 1: [None, REST[2][0], None, REST[2][1]],
               2: [None, REST[3][0], None, REST[3][1]], 3: []}
AFTER_PAIRS, AFTER_TURN, AFTER_LAYER1 = REST[2][2:3], REST[2][3:4], REST[2][4:]
AFTER_LAYER2, AFTER_LAYER3, LAST_GROUPS = REST[3][2:3], REST[3][3:4], REST[3][4:]
BEFORE_GRAM = {0: REST[0], 1: REST[1][NCH:], 2: AFTER_LAYER1, 3: LAST_GROUPS}


def gram_groups(t):
    return [("group", *k) for k in BEFORE_GRAM[t] + BESIDE_GRAM[t] if k]


def turn_fills(h):
    return [("turn", h, k) for k in range(KT)]


LOOK_ORDER = [("dense",)] + [("group", *k) for k in EARLY] + gram_groups(0) + gram_groups(1)
LOOK_ORDER += [("group", *k) for k in AFTER_PAIRS] + turn_fills(0) + [("group", *k) for k in AFTER_TURN]
LOOK_ORDER += gram_groups(2) + [("layer2", 0, n) for n in range(N2)]
LOOK_ORDER += [("group", *k) for k in AFTER_LAYER2 + AFTER_LAYER3]
LOOK_ORDER += gram_groups(3) + turn_fills(1) + [("layer2", 1, n) for n in range(N2)]
LOOK = {what: n for n, what in enumerate(LOOK_ORDER)}
assert FIRST_TABLE == 1 and all(("group", *k) in LOOK for k in ALL_GROUPS)


def look_on_act(what):
    return what[0] == "layer2" or (what[0] == "group" and what[2] % 2 == 1)


LOOK_ACT = [w for w in LOOK_ORDER if look_on_act(w)]
LOOK_DVE = [w for w in LOOK_ORDER if not look_on_act(w)]

LATE_ORDER = [("table", i) for i in range(NOH)]
for _h in range(HALVES):
    LATE_ORDER += [("layer1", _h, 0), ("layer1", _h, 1), ("layer3", _h)]
LATE = {what: n for n, what in enumerate(LATE_ORDER)}


def late_on_act(what):
    return what[0] == "table"


LATE_ACT = [w for w in LATE_ORDER if late_on_act(w)]
LATE_DVE = [w for w in LATE_ORDER if not late_on_act(w)]

PAIR_BANKS = 4
PAIR_NEED = [max(k for k in range(NB2) if BLOCK_OFF[BANKS2[k][0]] < (kt + 1) * P) for kt in range(KT)]
ROWS_OUT = 3 * 32 + NF


def build(nc, dense, ids_rows, ids_bcast, tables, w1, w2, b2, w3, out):
    with ExitStack() as ctx:
        def sb(name, shape, dt=F32):
            return ctx.enter_context(nc.sbuf_tensor(name, shape, dt))

        def sem(name):
            return ctx.enter_context(nc.semaphore(name))

        idx = sb("idx", [P, TILES, NTAB], I32)
        ids = sb("ids", [P, IDS_RING, B], I32)
        row0 = {c: sb(f"row_of_partition_{c}", [P, c]) for c in sorted(set(CHUNKS))}
        x_rows = sb("x_rows", [P, TILES, P])
        e_rows = sb("e_rows", [P, 2, NG, P])
        table = sb("table", [P, 2, MAXC, P])
        table_hi = sb("table_hi", [P, 2, MAXC, P], F32R)
        table_lo = sb("table_lo", [P, 2, MAXC, P], F32R)
        onehot = sb("onehot", [P, OH_RING, B], F32R)
        distance = sb("distance", [P, 2, B])
        eT = sb("eT", [P, B, SLOTS])
        x_hi = sb("x_hi", [P, B], F32R)
        x_lo = sb("x_lo", [P, B], F32R)
        dots = sb("dots", [P, NG_COL, HQ])
        pair_rows = sb("pair_rows", [HQ, QUADS, NPAIR])
        pT_hi = sb("pT_hi", [P, KT, HB], F32R)
        pT_lo = sb("pT_lo", [P, KT, HB], F32R)
        w1_raw = sb("w1_raw", [P, K1 + 1, H1])
        w1_hi = sb("w1_hi", [P, K1, H1], F32R)
        w1_lo = sb("w1_lo", [P, K1, H1], F32R)
        w2_raw = sb("w2_raw", [P, N1, H2])
        w2_hi = sb("w2_hi", [P, N1, H2], F32R)
        w2_lo = sb("w2_lo", [P, N1, H2], F32R)
        w3_sb = sb("w3_sb", [P, N2])
        b2_sb = sb("b2_sb", [P, N2])
        h1_hi = onehot[:, 0:2, :].rearrange("p a (k b) -> p (a k) b", b=HB)
        h1_lo = onehot[:, 2:4, :].rearrange("p a (k b) -> p (a k) b", b=HB)
        h2 = sb("h2", [P, N2, HB])
        y = sb("y", [1, B])
        ident = sb("ident", [P, P])
        one_col = sb("one_col", [P, P])

        look = ctx.enter_context(nc.psum_tensor("look", [P, 2, B], F32))
        gram = ctx.enter_context(nc.psum_tensor("gram", [P, 2, CHUNK_Q, P], F32))
        late = ctx.enter_context(nc.psum_tensor("late", [P, 2, B], F32))

        idx_in = sem("idx_in")
        ids_in = [sem(f"ids_in{k}") for k in range(IDS_RING)]
        table0_in = [sem(f"table0_in{k}") for k in range(2)]
        table_in = [sem(f"table_in{k}") for k in range(2)]
        x_in = sem("x_in")
        w_in = sem("w_in")
        rows_in = [[sem(f"rows_in{t}_{g}") for g in range(NGR)] for t in range(TILES)]
        y_out = sem("y_out")
        ident_ready = sem("ident_ready")
        row0_ready = sem("row0_ready")
        pads_ready = sem("pads_ready")
        bias_one = sem("bias_one")
        hi_ready = sem("hi_ready")
        lo_ready = sem("lo_ready")
        distance_ready = sem("distance_ready")
        pair_full = sem("pair_full")
        pair_act = sem("pair_act")
        pair_dve = sem("pair_dve")
        onehot_act = sem("onehot_act")
        onehot_dve = sem("onehot_dve")
        onehot_used = sem("onehot_used")
        look_full = sem("look_full")
        look_act = sem("look_act")
        look_dve = sem("look_dve")
        x_hi_ready = sem("x_hi_ready")
        w_sum = sem("w_sum")
        w_hi = sem("w_hi")
        w_lo = sem("w_lo")
        gram_full = sem("gram_full")
        dots_act = sem("dots_act")
        dots_dve = sem("dots_dve")
        late_full = sem("late_full")
        late_act = sem("late_act")
        late_dve = sem("late_dve")
        pT_hi_ready = sem("pT_hi_ready")
        h1_hi_ready = sem("h1_hi_ready")

        block = ctx.enter_context(nc.Block())

        def wait_look_done(eng, what):
            if look_on_act(what):
                eng.wait_ge(look_act, LOOK_ACT.index(what) + 1)
            else:
                eng.wait_ge(look_dve, LOOK_DVE.index(what) + 1)

        def wait_look_full(eng, what):
            eng.wait_ge(look_full, LOOK[what] + 1)

        def wait_late_done(eng, what):
            if late_on_act(what):
                eng.wait_ge(late_act, LATE_ACT.index(what) + 1)
            else:
                eng.wait_ge(late_dve, LATE_DVE.index(what) + 1)

        def wait_pairs_done(eng, h, k):
            fills = h * NB2 + k + 1
            odd = h * (NB2 // 2) + (k + 1) // 2
            eng.wait_ge(pair_act, fills - odd)
            if odd:
                eng.wait_ge(pair_dve, odd)

        def wait_late_full(eng, what):
            eng.wait_ge(late_full, LATE[what] + 1)

        def wait_onehot_free(eng, free):
            if free < 0:
                return
            k = max(a for a in range(NOH) if CHUNK0[a] <= free)
            if free == CHUNK0[k + 1] - 1:
                wait_late_full(eng, ("table", k))
            else:
                eng.wait_ge(onehot_used, free + 1 - k)

        @block.sync
        def _(sp):
            def load_table(i):
                c = CHUNKS[i]
                if i >= 2:
                    sp.wait_ge(lo_ready, pieces_split(i - 2))
                sp.dma_start(table[0:KP, i % 2, 0:c, :],
                             tables[ONE_HOT[i]].rearrange("(p c) d -> p c d", c=c)).then_inc(table_in[i % 2], 16)

            def load_ids(i):
                if i >= IDS_RING:
                    sp.wait_ge(onehot_dve, chunks_made(DVE_CHUNK, i - IDS_RING))
                    sp.wait_ge(onehot_act, chunks_made(ACT_CHUNK, i - IDS_RING))
                sp.dma_start(ids[:, i % IDS_RING, :], ids_bcast[ONE_HOT[i]:ONE_HOT[i] + 1, :].to_broadcast([P, B])
                             ).then_inc(ids_in[i % IDS_RING], 16)

            for k, (a, c) in enumerate(PIECES[0]):
                sp.dma_start(table[0:KP, 0, a:c, :], tables[ONE_HOT[0]].rearrange(
                    "(p c) d -> p c d", c=CHUNKS[0])[:, a:c, :]).then_inc(table0_in[k], 16)
            load_ids(1)
            load_table(1)
            sp.dma_start(x_rows[:, :, :], dense.rearrange("(t p) d -> p t d", p=P)).then_inc(x_in, 16)
            load_ids(2)
            load_ids(3)
            for i in range(2, NOH):
                load_table(i)
                if i + 2 < NOH:
                    load_ids(i + 2)
                if i == NOH - 1:
                    sp.dma_start(w1_raw[:, :, :], w1).then_inc(w_in, 16)
                    sp.dma_start(w2_raw[:, :, :], w2).then_inc(w_in, 16)
                    sp.dma_start(b2_sb[:, :], b2).then_inc(w_in, 16)
                    sp.dma_start(w3_sb[:, :], w3).then_inc(w_in, 16)
            wait_late_done(sp, ("layer3", HALVES - 1))
            sp.dma_start(out, y[:, :]).then_inc(y_out, 16)
            sp.wait_ge(y_out, 16)

        @block.gpsimd
        def _(pool):
            for c in sorted(row0):
                pool.iota(row0[c][:, :], pattern=[[1, c]], base=0, channel_multiplier=c,
                          allow_small_or_imprecise_dtypes=True).then_inc(row0_ready, 1)
            pool.memset(one_col[:, :], 1.0).then_inc(ident_ready, 1)
            pool.wait_ge(ident_ready, 1)
            pool.affine_select(out=ident[:, :], in_=one_col[:, :], compare_op=ALU.is_equal, fill=0.0,
                               base=0, pattern=[[-1, P]], channel_multiplier=1).then_inc(ident_ready, 1)
            pool.memset(pair_rows[:, :, NPAIR - 1:NPAIR], 1.0).then_inc(bias_one, 1)
            pool.wait_ge(idx_in, 16)
            for t, g in ALL_GROUPS:
                if t >= 2:
                    wait_look_full(pool, ("group", t - 2, g))
                for s in GROUPS[g]:
                    f = GATHERED[s]
                    pool.indirect_dma_start(
                        out=e_rows[:, t % 2, s, :], out_offset=None, in_=tables[f][:, :],
                        in_offset=bass.IndirectOffsetOnAxis(ap=idx[:, t, f:f + 1], axis=0)
                    ).then_inc(rows_in[t][g], 16)

        def pair_bank(k):
            bank = k % PAIR_BANKS
            return gram[:, bank // 2, bank % 2 * 4:bank % 2 * 4 + 4, :]

        eT_flat = eT[:, :, :].rearrange("d b s -> d (b s)")

        @block.tensor
        def _(pe):
            def look_bank(what):
                n = LOOK[what]
                if n >= 2:
                    wait_look_done(pe, LOOK_ORDER[n - 2])
                return look[:, n % 2, :]

            def late_bank(what):
                n = LATE[what]
                if n >= 2:
                    wait_late_done(pe, LATE_ORDER[n - 2])
                return late[:, n % 2, :]

            def turn_dense():
                pe.wait_ge(ident_ready, 2)
                pe.wait_ge(x_in, 16)
                bank = look_bank(("dense",))
                for t in range(TILES):
                    last = pe.transpose(bank[:, t * P:(t + 1) * P], x_rows[:, t, :], ident[:, :])
                last.then_inc(look_full, 1)

            def one_hot_product(i):
                bank = late_bank(("table", i))
                for c in range(CHUNKS[i]):
                    if c in [a for a, _ in PIECES[i]]:
                        pe.wait_ge(hi_ready, pieces_split(i, c))
                        pe.wait_ge(lo_ready, pieces_split(i, c))
                    if (i, c) in ACT_CHUNK:
                        pe.wait_ge(onehot_act, ACT_CHUNK.index((i, c)) + 1)
                    else:
                        pe.wait_ge(onehot_dve, DVE_CHUNK.index((i, c)) + 1)
                    hot = onehot[0:KP, (CHUNK0[i] + c) % OH_RING, :]
                    pe.matmul(bank, table_hi[0:KP, i % 2, c, :], hot, start=c == 0, stop=False)
                    last = pe.matmul(bank, table_lo[0:KP, i % 2, c, :], hot, start=False, stop=c == CHUNKS[i] - 1)
                    if c < CHUNKS[i] - 1:
                        last.then_inc(onehot_used, 1)
                last.then_inc(late_full, 1)

            def turn_group(t, g):
                bank = look_bank(("group", t, g))
                pe.wait_ge(rows_in[t][g], 16 * len(GROUPS[g]))
                for k, s in enumerate(GROUPS[g]):
                    last = pe.transpose(bank[:, k * P:(k + 1) * P], e_rows[:, t % 2, s, :], ident[:, :])
                last.then_inc(look_full, 1)

            def gram_tile(t):
                upto = LOOK["group", t, NGR - 1]
                if t == 0:
                    wait_late_done(pe, ("table", NOH - 1))
                    pe.wait_ge(pads_ready, 1)
                pe.wait_ge(look_act, len([w for w in LOOK_ACT if LOOK[w] <= upto]))
                pe.wait_ge(look_dve, len([w for w in LOOK_DVE if LOOK[w] <= upto]))
                if t == 2:
                    wait_pairs_done(pe, 0, NB2 - 1)
                for c in range(NCH):
                    n = t * NCH + c
                    if n >= 2:
                        pe.wait_ge(dots_act, n - 1)
                        pe.wait_ge(dots_dve, n - 1)
                    for q in range(CHUNK_Q):
                        b = t * P + (c * CHUNK_Q + q) * QUADS
                        last = pe.matmul(gram[0:ROWS_OUT, n % 2, q, 0:QUADS * NG_COL],
                                         eT_flat[:, b * SLOTS:b * SLOTS + ROWS_OUT],
                                         eT[:, b:b + QUADS, 0:NG_COL], start=True, stop=True)
                    last.then_inc(gram_full, 1)
                    if c < len(BESIDE_GRAM[t]) and BESIDE_GRAM[t][c]:
                        turn_group(*BESIDE_GRAM[t][c])

            def pairs_half(h):
                pe.wait_ge(dots_act, 2 * (h + 1) * NCH)
                pe.wait_ge(dots_dve, 2 * (h + 1) * NCH)
                for k, blocks in enumerate(BANKS2):
                    if k >= PAIR_BANKS:
                        wait_pairs_done(pe, h, k - PAIR_BANKS)
                    bank = pair_bank(k)
                    g0, g1 = BLOCKS[blocks[0]][0], sum(BLOCKS[blocks[-1]])
                    for g in range(g0, g1):
                        last = pe.transpose(bank[0:HQ, g - g0, 0:ROWS_OUT], dots[0:ROWS_OUT, g, :],
                                            ident[0:ROWS_OUT, 0:ROWS_OUT])
                    last.then_inc(pair_full, 1)

            def turn_pairs(h, k):
                bank = look_bank(("turn", h, k))
                pe.wait_ge(bias_one, 1)
                wait_pairs_done(pe, h, PAIR_NEED[k])
                for j in range(QUADS):
                    last = pe.transpose(bank[:, j * HQ:(j + 1) * HQ], pair_rows[:, j, k * P:(k + 1) * P],
                                        ident[0:HQ, 0:HQ])
                last.then_inc(look_full, 1)

            def layer1_tile(bank, n, k, hi, lo, first, last_one):
                o = bank[:, (n % 2) * HB:(n % 2 + 1) * HB]
                rows = slice(n * P, (n + 1) * P)
                pe.matmul(o, w1_hi[:, k, rows], hi, start=first, stop=False, skip_group_check=True)
                pe.matmul(o, w1_hi[:, k, rows], lo, start=False, stop=False, skip_group_check=True)
                return pe.matmul(o, w1_lo[:, k, rows], hi, start=False, stop=last_one, skip_group_check=True)

            def layer1_dense(h):
                if h == 0:
                    pe.wait_ge(w_hi, 1)
                    pe.wait_ge(w_lo, 1)
                cols = slice(h * HB, (h + 1) * HB)
                for i in range(2):
                    bank = late_bank(("layer1", h, i))
                    for n in (2 * i, 2 * i + 1):
                        layer1_tile(bank, n, KT, x_hi[:, cols], x_lo[:, cols], n % 2 == 0, False)

            def layer1_pairs(h):
                def step(i, k):
                    bank = late[:, LATE["layer1", h, i] % 2, :]
                    wait_look_done(pe, ("turn", h, k))
                    for n in (2 * i, 2 * i + 1):
                        last = layer1_tile(bank, n, k, pT_hi[:, k, :], pT_lo[:, k, :], False, k == KT - 1)
                    return last

                step(0, 0)
                step(1, 0)
                for i in range(2):
                    for k in range(1, KT):
                        last = step(i, k)
                    last.then_inc(late_full, 1)

            def layer2(h):
                if h == 0:
                    pe.wait_ge(w_hi, 2)
                    pe.wait_ge(w_lo, 2)
                banks = [look_bank(("layer2", h, n)) for n in range(N2)]

                def step(n, k):
                    o = banks[n][:, 0:HB]
                    rows = slice(n * P, (n + 1) * P)
                    pe.matmul(o, w2_hi[:, k, rows], h1_hi[:, k, :], start=k == 0, stop=False)
                    pe.matmul(o, w2_hi[:, k, rows], h1_lo[:, k, :], start=False, stop=False)
                    return pe.matmul(o, w2_lo[:, k, rows], h1_hi[:, k, :], start=False, stop=k == N1 - 1)

                wait_late_done(pe, ("layer1", h, 0))
                for n in range(N2):
                    for k in (0, 1):
                        step(n, k)
                wait_late_done(pe, ("layer1", h, 1))
                for n in range(N2):
                    for k in (2, 3):
                        last = step(n, k)
                    last.then_inc(look_full, 1)

            def layer3(h):
                bank = late_bank(("layer3", h))
                for k in range(N2):
                    wait_look_done(pe, ("layer2", h, k))
                    last = pe.matmul(bank[0:1, 0:HB], w3_sb[:, k:k + 1], h2[:, k, :], start=k == 0, stop=k == N2 - 1)
                last.then_inc(late_full, 1)

            def groups(ks):
                for k in ks:
                    turn_group(*k)

            pe.wait_ge(ident_ready, 2)
            for _ in range(WARM_UP):
                pe.matmul(gram[:, 0, 0, :], ident[:, :], ident[:, :], start=True, stop=True)
            for i in range(NOH):
                one_hot_product(i)
                if i >= FIRST_TABLE:
                    turn_group(*EARLY[i - FIRST_TABLE])
                else:
                    turn_dense()
            groups(BEFORE_GRAM[0])
            gram_tile(0)
            groups(BEFORE_GRAM[1])
            layer1_dense(0)
            gram_tile(1)
            pairs_half(0)
            groups(AFTER_PAIRS)
            for k in range(KT):
                turn_pairs(0, k)
            groups(AFTER_TURN)
            layer1_pairs(0)
            groups(BEFORE_GRAM[2])
            gram_tile(2)
            layer2(0)
            groups(AFTER_LAYER2)
            layer3(0)
            groups(AFTER_LAYER3)
            layer1_dense(1)
            groups(BEFORE_GRAM[3])
            gram_tile(3)
            pairs_half(1)
            for k in range(KT):
                turn_pairs(1, k)
            layer1_pairs(1)
            layer2(1)
            layer3(1)

        def group_copy(eng, copy, t, g, done):
            what = ("group", t, g)
            n = len(GROUPS[g])
            wait_look_full(eng, what)
            s = 1 + GROUPS[g][0]
            copy(eT[:, t * P:(t + 1) * P, s:s + n].rearrange("d b f -> d f b"),
                 look[:, LOOK[what] % 2, 0:n * P].rearrange("d (f b) -> d f b", f=n)).then_inc(done, 1)

        def dots_copy(copy, t, c, j):
            n = t * NCH + c
            rows = slice(32 * j, min(32 * j + 32, ROWS_OUT))
            q0 = (t % 2) * Q + c * CHUNK_Q
            return copy(dots[rows, :, q0:q0 + CHUNK_Q].rearrange("f g q -> f q g"),
                        gram[rows, n % 2, :, j * NG_COL:(j + 1) * NG_COL])

        def pair_copy(copy, k):
            first = BLOCKS[BANKS2[k][0]][0]
            for blk in BANKS2[k]:
                g0, ng = BLOCKS[blk]
                src = pair_bank(k)[0:HQ, g0 - first:g0 - first + ng, :].rearrange(
                    "q g (j f) -> q g j f", j=QUADS)[:, :, :, g0 + 1:NF]
                dst = pair_rows[:, :, BLOCK_OFF[blk]:BLOCK_OFF[blk + 1]].rearrange(
                    "q j (g w) -> q g j w", g=ng)
                last = copy(dst, src)
            return last

        def turned(h, k):
            src = look[:, LOOK["turn", h, k] % 2, 0:HB].rearrange("p (j q) -> p j q", j=QUADS)
            return [src] + [t[:, k, :].rearrange("p (q j) -> p j q", j=QUADS) for t in (pT_hi, pT_lo)]

        @block.scalar
        def _(act):
            def copy(dst, src):
                return act.activation(dst, src, ACT.Copy)

            def split_hi(i):
                if i >= 2:
                    wait_late_full(act, ("table", i - 2))
                for k, (a, c) in enumerate(PIECES[i]):
                    if i == 0:
                        act.wait_ge(table0_in[k], 16)
                    else:
                        act.wait_ge(table_in[i % 2], 16 * (i // 2 + i % 2))
                    copy(table_hi[0:KP, i % 2, a:c, :], table[0:KP, i % 2, a:c, :]).then_inc(hi_ready, 1)

            def one_hot(i, c):
                n = ACT_CHUNK.index((i, c))
                free = CHUNK0[i] + c - OH_RING
                act.activation(distance[0:KP, n % 2, :], ids[0:KP, i % IDS_RING, :], ACT.Abs,
                               bias=row0[CHUNKS[i]][0:KP, c:c + 1], scale=-1.0).then_inc(distance_ready, 1)
                wait_onehot_free(act, free)
                act.wait_ge(distance_ready, n + 1)
                act.activation(onehot[0:KP, (free + OH_RING) % OH_RING, :], distance[0:KP, n % 2, :], ACT.Relu,
                               bias=1.0, scale=-1.0).then_inc(onehot_act, 1)

            def table_copy(i):
                wait_late_full(act, ("table", i))
                copy(eT[:, :, 1 + NG + i], late[:, LATE["table", i] % 2, :]).then_inc(late_act, 1)

            act.dma_start(idx[:, :, :], ids_rows).then_inc(idx_in, 16)
            act.dma_start(ids[:, 0, :], ids_bcast[ONE_HOT[0]:ONE_HOT[0] + 1, :].to_broadcast([P, B])
                          ).then_inc(ids_in[0], 16)
            act.wait_ge(row0_ready, len(row0))
            split_hi(0)

            def groups(ks):
                for k in ks:
                    if look_on_act(("group", *k)):
                        group_copy(act, copy, *k, look_act)

            def one_hots(i, c):
                if i < NOH:
                    if c == ACT_CHUNK[0][1]:
                        act.wait_ge(ids_in[i % IDS_RING], 16 * (i // IDS_RING + 1))
                    one_hot(i, c)

            one_hots(0, 3)
            one_hots(0, 7)
            for i in range(NOH):
                if i + 1 < NOH:
                    split_hi(i + 1)
                if i:
                    one_hots(i, 7)
                one_hots(i + 1, 3)
                if i == 1:
                    wait_look_full(act, ("dense",))
                    bank = look[:, LOOK["dense",] % 2, :]
                    copy(eT[:, :, 0], bank)
                    copy(x_hi[:, :], bank).then_inc(x_hi_ready, 1)
                if i >= 1:
                    table_copy(i - 1)
                if i - 1 >= FIRST_TABLE:
                    groups([EARLY[i - 1 - FIRST_TABLE]])
            table_copy(NOH - 1)
            groups(EARLY[-1:])

            act.wait_ge(w_in, 16 * 4)
            act.wait_ge(w_sum, 1)
            copy(w1_hi[:, :, :], w1_raw[:, 0:K1, :]).then_inc(w_hi, 1)

            def dots_tile(t):
                if t == 2:
                    act.wait_ge(pair_full, NB2)
                for c in range(NCH):
                    act.wait_ge(gram_full, t * NCH + c + 1)
                    dots_copy(copy, t, c, 0)
                    dots_copy(copy, t, c, 1).then_inc(dots_act, 1)
                    groups([k for k in BESIDE_GRAM[t][c:c + 1] if k])

            def pairs_half(h):
                if h:
                    wait_look_full(act, ("turn", h - 1, KT - 1))
                for k in range(0, NB2, 2):
                    act.wait_ge(pair_full, h * NB2 + k + 1)
                    pair_copy(copy, k).then_inc(pair_act, 1)

            def turn_hi(h):
                if h:
                    wait_late_full(act, ("layer1", h - 1, 1))
                for k in range(KT):
                    wait_look_full(act, ("turn", h, k))
                    src, hi, _ = turned(h, k)
                    copy(hi, src).then_inc(pT_hi_ready, 1)

            def h1_split(h):
                if h:
                    wait_look_full(act, ("layer2", h - 1, N2 - 1))
                for i in range(2):
                    wait_late_full(act, ("layer1", h, i))
                    act.activation(h1_hi[:, 2 * i:2 * i + 2, :], late[:, LATE["layer1", h, i] % 2, :].rearrange(
                        "n (k b) -> n k b", k=2), ACT.Relu).then_inc(h1_hi_ready, 1)

            def h2_relu(h):
                if h:
                    wait_late_full(act, ("layer3", h - 1))
                for n in range(N2):
                    wait_look_full(act, ("layer2", h, n))
                    act.activation(h2[:, n, :], look[:, LOOK["layer2", h, n] % 2, 0:HB],
                                   ACT.Relu, bias=b2_sb[:, n:n + 1]).then_inc(look_act, 1)

            groups(BEFORE_GRAM[0])
            dots_tile(0)
            copy(w2_hi[:, :, :], w2_raw[:, :, :]).then_inc(w_hi, 1)
            groups(BEFORE_GRAM[1])
            dots_tile(1)
            pairs_half(0)
            groups(AFTER_PAIRS)
            turn_hi(0)
            groups(AFTER_TURN)
            h1_split(0)
            groups(BEFORE_GRAM[2])
            dots_tile(2)
            h2_relu(0)
            groups(AFTER_LAYER2 + AFTER_LAYER3 + BEFORE_GRAM[3])
            dots_tile(3)
            pairs_half(1)
            turn_hi(1)
            h1_split(1)
            h2_relu(1)

        @block.vector
        def _(dve):
            copy = dve.tensor_copy

            def split_lo(i):
                for a, c in PIECES[i]:
                    dve.wait_ge(hi_ready, pieces_split(i, a))
                    dve.tensor_tensor(table_lo[0:KP, i % 2, a:c, :], table[0:KP, i % 2, a:c, :],
                                      table_hi[0:KP, i % 2, a:c, :].bitcast(F32), ALU.subtract
                                      ).then_inc(lo_ready, 1)

            def one_hot(i, c):
                n = CHUNK0[i] + c
                wait_onehot_free(dve, n - OH_RING)
                dve.tensor_scalar(onehot[0:KP, n % OH_RING, :], ids[0:KP, i % IDS_RING, :],
                                  row0[CHUNKS[i]][0:KP, c:c + 1], None, ALU.is_equal).then_inc(onehot_dve, 1)

            dve.memset(eT[:, :, NF:SLOTS], 0.0).then_inc(pads_ready, 1)
            dve.wait_ge(row0_ready, len(row0))

            def groups(ks):
                for k in ks:
                    if not look_on_act(("group", *k)):
                        group_copy(dve, copy, *k, look_dve)

            def one_hots(i, mine):
                for c in mine:
                    one_hot(i, c)

            mine = [c for a, c in DVE_CHUNK if a == 0]
            dve.wait_ge(ids_in[0], 16)
            one_hots(0, mine[:2])
            split_lo(0)
            one_hots(0, mine[2:])
            for i in range(NOH):
                if i + 1 < NOH:
                    split_lo(i + 1)
                    dve.wait_ge(ids_in[(i + 1) % IDS_RING], 16 * ((i + 1) // IDS_RING + 1))
                    one_hots(i + 1, [c for a, c in DVE_CHUNK if a == i + 1])
                if i == 1:
                    dve.wait_ge(x_hi_ready, 1)
                    dve.tensor_tensor(x_lo[:, :], look[:, LOOK["dense",] % 2, :], x_hi[:, :].bitcast(F32),
                                      ALU.subtract).then_inc(look_dve, 1)
                if i - 1 >= FIRST_TABLE:
                    groups([EARLY[i - 1 - FIRST_TABLE]])
            dve.wait_ge(w_in, 16 * 4)
            dve.tensor_tensor(w1_raw[:, KT, :], w1_raw[:, KT, :], w1_raw[:, KT + 1, :], ALU.add
                              ).then_inc(w_sum, 1)
            groups(EARLY[-1:])

            def dots_tile(t):
                if t == 2:
                    dve.wait_ge(pair_full, NB2)
                for c in range(NCH):
                    dve.wait_ge(gram_full, t * NCH + c + 1)
                    dots_copy(copy, t, c, 2)
                    dots_copy(copy, t, c, 3).then_inc(dots_dve, 1)
                    groups([k for k in BESIDE_GRAM[t][c:c + 1] if k])

            def pairs_half(h):
                if h:
                    wait_look_full(dve, ("turn", h - 1, KT - 1))
                for k in range(1, NB2, 2):
                    dve.wait_ge(pair_full, h * NB2 + k + 1)
                    pair_copy(copy, k).then_inc(pair_dve, 1)

            def turn_lo(h):
                for k in range(KT):
                    dve.wait_ge(pT_hi_ready, KT * h + k + 1)
                    src, hi, lo = turned(h, k)
                    dve.tensor_tensor(lo, src, hi.bitcast(F32), ALU.subtract).then_inc(look_dve, 1)

            def h1_rest(h):
                for i in range(2):
                    dve.wait_ge(h1_hi_ready, 2 * h + i + 1)
                    rows = slice(2 * i, 2 * i + 2)
                    dve.scalar_tensor_tensor(out=h1_lo[:, rows, :],
                                             in0=late[:, LATE["layer1", h, i] % 2, :].rearrange(
                                                 "n (k b) -> n k b", k=2),
                                             scalar=0.0, in1=h1_hi[:, rows, :].bitcast(F32),
                                             op0=ALU.max, op1=ALU.subtract).then_inc(late_dve, 1)

            def y_copy(h):
                wait_late_full(dve, ("layer3", h))
                copy(y[0:1, h * HB:(h + 1) * HB], late[0:1, LATE["layer3", h] % 2, 0:HB]).then_inc(late_dve, 1)

            groups(BEFORE_GRAM[0])
            dve.wait_ge(w_hi, 1)
            dve.tensor_tensor(w1_lo[:, :, :], w1_raw[:, 0:K1, :], w1_hi[:, :, :].bitcast(F32), ALU.subtract
                              ).then_inc(w_lo, 1)
            dots_tile(0)
            groups(BEFORE_GRAM[1])
            dots_tile(1)
            dve.wait_ge(w_hi, 2)
            dve.tensor_tensor(w2_lo[:, :, :], w2_raw[:, :, :], w2_hi[:, :, :].bitcast(F32), ALU.subtract
                              ).then_inc(w_lo, 1)
            pairs_half(0)
            groups(AFTER_PAIRS)
            turn_lo(0)
            groups(AFTER_TURN)
            h1_rest(0)
            groups(BEFORE_GRAM[2])
            dots_tile(2)
            groups(AFTER_LAYER2)
            y_copy(0)
            groups(AFTER_LAYER3 + BEFORE_GRAM[3])
            dots_tile(3)
            pairs_half(1)
            turn_lo(1)
            h1_rest(1)
            y_copy(1)


def kernel(**inputs):
    import numpy as np
    import concourse.bacc as bacc
    from concourse.bass_utils import run_bass_kernel_spmd

    ids = np.ascontiguousarray(inputs["ids"])
    w1 = np.ascontiguousarray(inputs["W_top1"])
    npairs = NF * (NF - 1) // 2
    w1_rows = np.zeros((NPAIR + 2 * P, H1), w1.dtype)
    w1_rows[NPAIR - 1] = inputs["b_top1"]
    for n, r in enumerate(pair_rows_of_w1()):
        if r is not None:
            w1_rows[n] = w1[r]
    w1_rows[NPAIR:NPAIR + P] = w1[0:P]
    w1_rows[NPAIR + P:] = w1[P + npairs:]
    arrays = {
        "dense": np.ascontiguousarray(inputs["r_dense_features"]),
        "ids_rows": np.ascontiguousarray(ids.reshape(TILES, P, NTAB).transpose(1, 0, 2)),
        "ids_bcast": np.ascontiguousarray(ids.T),
        "w1": np.ascontiguousarray(w1_rows.reshape(K1 + 1, P, H1).transpose(1, 0, 2)),
        "w2": np.ascontiguousarray(np.asarray(inputs["W_top2"]).reshape(N1, P, H2).transpose(1, 0, 2)),
        "b2": np.ascontiguousarray(np.asarray(inputs["b_top2"]).reshape(N2, P).T),
        "w3": np.ascontiguousarray(np.asarray(inputs["W_top3"]).reshape(N2, P).T),
    }
    for f in range(NTAB):
        arrays[f"tbl_{f}"] = np.ascontiguousarray(inputs[f"tbl_{f}"])

    nc = bacc.Bacc("TRN2", target_bir_lowering=False, num_devices=1)
    ap = {name: nc.dram_tensor(f"in_{name}", a.shape, mybir.dt.from_np(a.dtype), kind="ExternalInput").ap()
          for name, a in arrays.items()}
    out = nc.dram_tensor("out_y", (1, B), F32, kind="ExternalOutput").ap()
    build(nc, ap["dense"], ap["ids_rows"], ap["ids_bcast"], [ap[f"tbl_{f}"] for f in range(NTAB)],
          ap["w1"], ap["w2"], ap["b2"], ap["w3"], out)
    r = run_bass_kernel_spmd(nc, [{f"in_{name}": a for name, a in arrays.items()}], core_ids=[0])
    return r.results[0]["out_y"].reshape(B, 1)
```
